# Optimizing a Trainium2 kernel written in Bass

```python
import numpy as np
import jax
import jax.numpy as jnp

def _softmax(x, axis=-1):
    return jax.nn.softmax(x, axis=axis)

def _gelu(x):
    return jax.nn.gelu(x, approximate=True)

def _silu(x):
    return jax.nn.silu(x)

def _sigmoid(x):
    return jax.nn.sigmoid(x)

def _layernorm(x, axis=-1, eps=1e-05):
    m = jnp.mean(x, axis=axis, keepdims=True)
    v = jnp.var(x, axis=axis, keepdims=True)
    return (x - m) / jnp.sqrt(v + eps)

def _scatter_add(tgt, idx, src, axis=0):
    return tgt.at[idx].add(src)

def _segment_sum(src, seg, n):
    return jax.ops.segment_sum(src, seg, n)
kernel_name = 'mk_seq_preln_d1_jaxref_r8_4bca52'

def setup_inputs(seed: int=0):
    np.random.seed(seed)
    _w = jnp.asarray

    def _L0_attn_setup():
        import jax, jax.numpy as jnp
        import numpy as np
        ROPE_BASE = 10000.0

        def _rope_tables(T, head_dim, dtype):
            inv_freq = 1.0 / ROPE_BASE ** (jnp.arange(0, head_dim, 2, dtype=jnp.float32) / head_dim)
            freqs = jnp.arange(T, dtype=jnp.float32)[:, None] * inv_freq[None, :]
            freqs = jnp.repeat(freqs, 2, axis=-1)
            return (jnp.cos(freqs).astype(dtype), jnp.sin(freqs).astype(dtype))

        def _rotate_half(x):
            x = x.reshape(x.shape[:-1] + (-1, 2))
            x1, x2 = (x[..., 0], x[..., 1])
            return jnp.stack((-x2, x1), axis=-1).reshape(x.shape[:-2] + (-1,))

        def _apply_rope(x, cos, sin):
            return x * cos[None, None] + _rotate_half(x) * sin[None, None]
        key = jax.random.key(seed)
        k1, k2, k3 = jax.random.split(key, 3)
        B, T, C = (4, 256, 128)
        x = jax.random.normal(k1, (B, T, C), dtype=jnp.float32)
        W_attn = jax.random.normal(k2, (C, 3 * C), dtype=jnp.float32) * 0.02
        W_proj = jax.random.normal(k3, (C, C), dtype=jnp.float32) * 0.02
        return {'x': x, 'W_attn': W_attn, 'W_proj': W_proj}
    _L0_attn_in = _L0_attn_setup()

    def _L0_ffn_setup():
        import jax, jax.numpy as jnp
        import numpy as np
        from jax.scipy.special import logsumexp
        EPS = 1e-06
        SINKHORN_ITERS = 8
        TEMPERATURE = 1.0

        def sinkhorn(logits):
            t = jnp.log(jnp.clip(logits, EPS)) / TEMPERATURE
            for _ in range(SINKHORN_ITERS):
                t = t - logsumexp(t, axis=-2, keepdims=True)
                t = t - logsumexp(t, axis=-1, keepdims=True)
            return jnp.exp(t)
        key = jax.random.key(seed)
        k1, k2, k3 = jax.random.split(key, 3)
        b, n, d, e, h = (4, 512, 128, 8, 1)
        x = jax.random.normal(k1, (b, n, d), dtype=jnp.float32)
        gate_w = jax.random.normal(k2, (h, d, e), dtype=jnp.float32)
        experts = jax.random.normal(k3, (e, d, d), dtype=jnp.float32) * 0.02
        return {'x': x, 'gate_w': gate_w, 'experts': experts}
    _L0_ffn_in = _L0_ffn_setup()
    _d = {'L0_attn_x': _L0_attn_in['x'], 'L0_attn_W_attn': _L0_attn_in['W_attn'], 'L0_attn_W_proj': _L0_attn_in['W_proj'], 'L0_ffn_gate_w': _L0_ffn_in['gate_w'], 'L0_ffn_experts': _L0_ffn_in['experts']}
    _x0 = _d['L0_attn_x']
    _d['L0_attn_x'] = jax.random.normal(jax.random.fold_in(jax.random.key(seed), 1), (8, 512, 128), dtype=_x0.dtype)
    del _x0
    return _d

def reference(L0_attn_x, L0_attn_W_attn, L0_attn_W_proj, L0_ffn_gate_w, L0_ffn_experts):

    def _L0_attn_ref(x, W_attn, W_proj):
        import jax, jax.numpy as jnp
        import numpy as np
        ROPE_BASE = 10000.0

        def _rope_tables(T, head_dim, dtype):
            inv_freq = 1.0 / ROPE_BASE ** (jnp.arange(0, head_dim, 2, dtype=jnp.float32) / head_dim)
            freqs = jnp.arange(T, dtype=jnp.float32)[:, None] * inv_freq[None, :]
            freqs = jnp.repeat(freqs, 2, axis=-1)
            return (jnp.cos(freqs).astype(dtype), jnp.sin(freqs).astype(dtype))

        def _rotate_half(x):
            x = x.reshape(x.shape[:-1] + (-1, 2))
            x1, x2 = (x[..., 0], x[..., 1])
            return jnp.stack((-x2, x1), axis=-1).reshape(x.shape[:-2] + (-1,))

        def _apply_rope(x, cos, sin):
            return x * cos[None, None] + _rotate_half(x) * sin[None, None]
        B, T, C = x.shape
        n_head = 16
        hd = C // n_head
        qkv = x @ W_attn
        q, k, v = jnp.split(qkv, 3, axis=-1)
        q = q.reshape(B, T, n_head, hd).transpose(0, 2, 1, 3)
        k = k.reshape(B, T, n_head, hd).transpose(0, 2, 1, 3)
        v = v.reshape(B, T, n_head, hd).transpose(0, 2, 1, 3)
        cos, sin = _rope_tables(T, hd, x.dtype)
        q = _apply_rope(q, cos, sin)
        k = _apply_rope(k, cos, sin)
        att = jnp.einsum('bhqd,bhkd->bhqk', q, k) * (1.0 / jnp.sqrt(jnp.array(hd, dtype=x.dtype)))
        causal = jnp.tril(jnp.ones((T, T), dtype=bool))
        att = jnp.where(causal[None, None], att, jnp.array(-jnp.inf, dtype=att.dtype))
        att = jax.nn.softmax(att, axis=-1)
        y = jnp.einsum('bhqk,bhkd->bhqd', att, v)
        y = y.transpose(0, 2, 1, 3).reshape(B, T, C)
        return y @ W_proj

    def _L0_ffn_ref(x, gate_w, experts):
        import jax, jax.numpy as jnp
        import numpy as np
        from jax.scipy.special import logsumexp
        EPS = 1e-06
        SINKHORN_ITERS = 8
        TEMPERATURE = 1.0

        def sinkhorn(logits):
            t = jnp.log(jnp.clip(logits, EPS)) / TEMPERATURE
            for _ in range(SINKHORN_ITERS):
                t = t - logsumexp(t, axis=-2, keepdims=True)
                t = t - logsumexp(t, axis=-1, keepdims=True)
            return jnp.exp(t)
        b, n, d = x.shape
        h, _, e = gate_w.shape
        m = n // e
        xh = x[:, None]
        gate_logits = jnp.einsum('bhnd,hde->bhne', xh, gate_w)
        gates = sinkhorn(gate_logits)
        g = jnp.swapaxes(gates, -1, -2)
        gv, idx = jax.lax.top_k(g, m)
        gate_values = jnp.swapaxes(gv, -1, -2)
        routed_indices = jnp.swapaxes(idx, -1, -2)
        hard_gates = (gate_values > 0.5).astype(x.dtype)
        bi = jnp.arange(b)[:, None, None, None]
        hi = jnp.arange(h)[None, :, None, None]
        routed = xh[bi, hi, routed_indices]
        experts4 = experts[:, None, :, :]
        out = jnp.einsum('bhmei,ehio->bhmeo', routed, experts4)
        out = out * hard_gates[..., None]
        y = jnp.zeros_like(xh).at[bi, hi, routed_indices].set(out)
        return y[:, 0]
    x = L0_attn_x
    x = x + _L0_attn_ref(_layernorm(x, axis=-1), L0_attn_W_attn, L0_attn_W_proj)
    x = x + _L0_ffn_ref(_layernorm(x, axis=-1), L0_ffn_gate_w, L0_ffn_experts)
    return x

_drawn_inputs = setup_inputs


def setup_inputs(seed=0):
    import zlib

    import numpy as np

    out = dict(_drawn_inputs(seed))
    spreads = {}
    factors = {'L0_attn_W_attn': 5.65, 'L0_attn_W_proj': 3.685}
    for name, (base, spread) in spreads.items():
        noise = np.random.default_rng([zlib.crc32(name.encode()), seed]).standard_normal(out[name].shape)
        drawn = base * np.exp(spread * noise) if base else spread * noise
        out[name] = jnp.asarray(drawn.astype(out[name].dtype))
    for name, factor in factors.items():
        out[name] = (out[name] * factor).astype(out[name].dtype)
    return out
```

```python
import numpy as np
import concourse.bass as bass
from concourse import mybir
from contextlib import ExitStack

F32 = mybir.dt.float32
BF16 = mybir.dt.bfloat16
U32 = mybir.dt.uint32
ACT = mybir.ActivationFunctionType
ALU = mybir.AluOpType
AX = mybir.AxisListType

B, T, C = 8, 512, 128
H, HD = 16, 8
E = 8
P = 128
TB = T // P
PAIRS = H // 2
TOPK = T // E
SINKHORN_ITERS = 8
LN_EPS = 1e-5
CLIP_EPS = 1e-6

Q_PART = [0, 0, 0, 1, 1, 2]
K_PART = [0, 1, 2, 0, 1, 0]
HEAD_ROWS = len(Q_PART) * HD
ROWS_K = 2 * HEAD_ROWS
MAX_ROW = ROWS_K
ALL_K = MAX_ROW + 4
VS = HD + 1
VKB = H * VS + 32

MISC = ["xnT n", "q n", "qs n", "ot3 p", "mx1",
        "k n", "ks n", "yT p", "v n", "ot0", "mx2",
        "proj p", "ot1", "mx3",
        "xn2T p", "logits p", "ot2", "mx0 n"]
MISC_START = ["xnT n", "q n", "qs n", "k n", "ks n", "v n", "mx0 n"]
MISC_END = ["ot3 p", "yT p", "proj p", "xn2T p", "logits p"]
PREV = sum(m.endswith("p") for m in MISC)
NEXT = sum(m.endswith("n") for m in MISC)


class Batch:

    def __init__(self, b, par, prev=True, nxt=True, order=MISC):
        self.b, self.par, self.prev, self.nxt = b, par, prev, nxt
        self.order = [m.split()[0] for m in order
                      if (prev or not m.endswith("p")) and (nxt or not m.endswith("n"))]
        if order is MISC_START:
            self.base = 0
        elif order is MISC_END:
            self.base = b * len(MISC) + len(MISC_START) - PREV - NEXT
        elif not prev:
            self.base = len(MISC_START)
        else:
            self.base = b * len(MISC) + (len(MISC_START) - PREV)

    def misc(self, name):
        return self.base + self.order.index(name)


def build(nc, x_in, w_qkv, w_swap, w_proj, gate_w, experts, rope, tri, ident, small, out):
    ctx = ExitStack()
    with ctx:
        def sb(name, shape, dt=F32):
            return ctx.enter_context(nc.sbuf_tensor(name, shape, dt))

        def sem(name):
            return ctx.enter_context(nc.semaphore(name))

        WQKV = sb("WQKV", [P, 3 * C])
        WSWAP = sb("WSWAP", [P, 2 * C])
        WPROJ = sb("WPROJ", [P, C])
        WGATE = sb("WGATE", [P, E])
        WEXP = sb("WEXP", [P, E, C])
        ROPE = sb("ROPE", [P, 4, T])
        TRI = sb("TRI", [P, T])
        IDF = sb("IDF", [P, P])
        IDB = sb("IDB", [P, P], BF16)
        SMALL = sb("SMALL", [P, T + 2 + E])
        RANKC = sb("RANKC", [P, 2], BF16)
        ONES = sb("ONES", [P, P])
        NHALF = sb("NHALF", [P, TB])
        ONER = sb("ONER", [2, PAIRS * T], BF16)
        X = sb("X", [P, B * TB, C])
        LG = sb("LG", [P, B * TB, E])
        QP = [sb(f"QP{i}", [P, PAIRS, T], BF16) for i in range(2)]
        KZ = [[sb(f"KZ{i}{h}", [P, PAIRS, T], BF16) for h in range(2)] for i in range(2)]
        VP = [sb(f"VP{i}", [P, TB * VKB]) for i in range(2)]
        PT = [sb(f"PT{i}", [P, 5, 2 * T]) for i in range(2)]
        XN = sb("XN", [P, TB, C])
        XNT = sb("XNT", [P, T])
        ST = sb("ST", [P, TB, 6])
        MV = sb("MV", [P, TB, 2])
        RSTD = sb("RSTD", [P, TB])
        TC = sb("TC", [P, T])
        TS = sb("TS", [P, T])
        RES = [sb(f"RES{w}", [P, T]) for w in range(2)]
        PARTS = [sb(f"PARTS{w}", [P, 3, T], BF16) for w in range(2)]
        MX = [sb(f"MX{i}", [P, 16]) for i in range(2)]
        NMX = sb("NMX", [P, 8, 2, 2], BF16)
        JUNK = [sb(f"JUNK{i}", [P, T], BF16) for i in range(2)]
        OT = sb("OT", [P, T])
        RSUM = sb("RSUM", [P, TB, 4])
        Y = sb("Y", [P, TB, C])
        YT = sb("YT", [P, T])
        XN2 = sb("XN2", [P, TB, C])
        ST2 = sb("ST2", [P, TB, 6])
        MV2 = sb("MV2", [P, TB, 2])
        RSTD2 = sb("RSTD2", [P, TB])
        XN2S = sb("XN2S", [P, T])
        KT = sb("KT", [P, B, TB, E])
        PROD = sb("PROD", [P, TB, B, E])
        SCALED = sb("SCALED", [P, B, TB, E])
        RINV = sb("RINV", [P, B * TB])
        RSC = sb("RSC", [P, B * TB])
        CSC = sb("CSC", [P, B, E])
        GT = sb("GT", [B * E, T])
        TOPV = sb("TOPV", [B * E, 8])
        TOPI8 = sb("TOPI8", [B * E, 8], U32)
        TOPF = sb("TOPF", [B * E, 2, TOPK])
        IT = sb("IT", [P, B * E // 2])
        OH = [sb(f"OH{i}", [P, T], BF16) for i in range(2)]
        KEY = sb("KEY", [P, B * TB, E])
        KMAX = sb("KMAX", [P, B * TB])
        HARD = sb("HARD", [P, B * TB, E])
        W = sb("W", [P, B * TB * E])
        XS = [sb(f"XS{i}", [P, T]) for i in range(2)]
        PA = [sb(f"PA{i}", [P, 4, C]) for i in range(2)]
        SS = [sb(f"SS{i}", [P, 4, C]) for i in range(2)]
        S2 = [sb(f"S2{i}", [P, 2, C]) for i in range(2)]
        O1 = [sb(f"O1{i}", [P, C]) for i in range(2)]
        OUTB = [sb(f"OUTB{i}", [P, TB, C]) for i in range(2)]

        CH = [ctx.enter_context(nc.psum_tensor(f"CH{i}", [P, 2 * T], F32)) for i in range(2)]
        ROWP = [ctx.enter_context(nc.psum_tensor(f"ROWP{i}", [P, T], F32)) for i in range(2)]
        PVB = ctx.enter_context(nc.psum_tensor("PVB", [P, T], F32))
        MB = ctx.enter_context(nc.psum_tensor("MB", [P, T], F32))
        MBH = MB[:, :].bitcast(BF16)
        MB4 = MB[:, :].rearrange("p (a c) -> p a c", a=TB)

        xn2_dram = nc.dram_tensor("xn2_scratch", [B, P, T], F32, kind="Internal").ap()
        scratch = nc.dram_tensor("parts_scratch", [2, 2, 2, 3, HD, PAIRS, T], BF16, kind="Internal").ap()

        ident_loaded = sem("ident_loaded")
        x_first = sem("x_first_loaded")
        x_rest = sem("x_rest_loaded")
        weights = sem("weights_loaded")
        built = sem("constants_built")
        one_rows = sem("one_rows_loaded")
        rows_ready = sem("score_rows_ready")
        row_max = sem("row_max_done")
        nmax_ready = sem("minus_max_ready")
        chunk_ready = sem("score_chunk_ready")
        exp_done = sem("exp_done")
        causal_done = sem("causal_done")
        pv_done = sem("pv_done")
        pv_copied = sem("pv_copied")
        misc_full = sem("misc_full")
        misc_free = sem("misc_free")
        ln_stats = sem("ln_stats")
        ln_rstd = sem("ln_rstd")
        xn_ready = sem("xn_ready")
        ln2_stats = sem("ln2_stats")
        ln2_rstd = sem("ln2_rstd")
        xn2_ready = sem("xn2_ready")
        resid = [sem("q_residual"), sem("k_residual")]
        part = [sem("q_part"), sem("k_part")]
        xn2_saved = sem("xn2_saved")
        stored = [sem("q_stored"), sem("k_stored")]
        loaded = [sem("q_loaded"), sem("k_loaded")]
        sink_prod = sem("sinkhorn_product")
        sink_sum = sem("sinkhorn_sum")
        gt_ready = sem("gates_transposed")
        topi_ready = sem("top_indices")
        it_ready = sem("indices_transposed")
        onehot = sem("onehot_ready")
        onehot_used = sem("onehot_used")
        w_ready = sem("weights_of_experts")
        xs_ready = [sem("xn2_even_loaded"), sem("xn2_odd_loaded")]
        y_full = sem("expert_outputs")
        pa_ready = sem("upper_experts_weighted")
        lower = sem("lower_experts_added")
        tile_out = sem("tile_out")
        out_saved = [sem("out_even_saved"), sem("out_odd_saved")]

        block = ctx.enter_context(nc.Block())

        def batches(eng, one):
            one(Batch(0, 0, prev=False))
            with eng.Fori(1, B - 2, 2) as i:
                one(Batch(i, 1))
                one(Batch(i + 1, 0))
            one(Batch(B - 1, 1, nxt=False))

        @block.sync
        def _(sp):
            xv = x_in.rearrange("b (t p) c -> b p t c", p=P)
            Xv = [X[:, TB * b:TB * b + TB, :] for b in range(B)]
            sp.dma_start(Xv[0], xv[0]).then_inc(x_first, 16)
            sp.dma_start(IDF[:, :], ident).then_inc(ident_loaded, 16)
            sp.dma_start(WQKV[:, :], w_qkv).then_inc(weights, 16)
            sp.dma_start(WSWAP[:, :], w_swap).then_inc(weights, 16)
            sp.dma_start(ROPE[:, :, :], rope).then_inc(weights, 16)
            sp.dma_start(TRI[:, :], tri).then_inc(weights, 16)
            sp.dma_start(WPROJ[:, :], w_proj).then_inc(weights, 16)
            sp.dma_start(WGATE[:, :], gate_w).then_inc(weights, 16)
            sp.dma_start(SMALL[:, :], small).then_inc(weights, 16)
            for b in range(1, B):
                sp.dma_start(Xv[b], xv[b]).then_inc(x_rest, 16)
            sp.dma_start(WEXP[:, :, :], experts.rearrange("e d o -> d e o")).then_inc(weights, 16)
            sp.wait_ge(built, 8)
            for i in range(2):
                for h in range(2):
                    r = MAX_ROW + 2 * h
                    sp.dma_start(KZ[i][h][r:r + 2, :, :].rearrange("p a t -> p (a t)"),
                                 ONER[:, :]).then_inc(one_rows, 16)

            def trip(b, par, w, used):
                sp.wait_ge(part[w], 3 * b + 3)
                if used:
                    sp.wait_ge(chunk_ready, 20 * b - 20)
                sc = scratch[w, par]
                for h in range(2):
                    sp.dma_start(sc[h].rearrange("n d a t -> (d a) n t"),
                                 PARTS[w][64 * h:64 * h + 64, :, :]).then_inc(stored[w], 16)
                sp.wait_ge(stored[w], 32 * b + 32)
                for h in range(2):
                    rows = (QP[par] if w == 0 else KZ[par][h])[:, :, :].rearrange("p a t -> p (a t)")
                    for i, n in ((0, 3), (1, 2), (2, 1)):
                        slot = Q_PART.index(i)
                        r = HEAD_ROWS * h + HD * slot
                        if w == 0:
                            src = sc[h, i].rearrange("d a t -> d (a t)")
                            src = bass.AP(tensor=src.tensor, offset=src.offset,
                                          ap=[[0, n]] + [list(x) for x in src.ap])
                        else:
                            src = sc[h, 0:n].rearrange("n d a t -> (n d) (a t)")
                        sp.dma_start(rows[r:r + HD * n, :], src).then_inc(loaded[w], 16)

            trip(0, 0, 0, False)
            trip(0, 0, 1, False)

            def one(bt):
                if bt.nxt:
                    trip(bt.b + 1, 1 - bt.par, 0, bt.prev)
                    trip(bt.b + 1, 1 - bt.par, 1, bt.prev)
                if bt.prev:
                    save_xn2(bt)

            def save_xn2(bt):
                sp.wait_ge(misc_free, bt.misc("xn2T") + 1)
                sp.dma_start(xn2_dram[bass.ds(bt.b - 1, 1), :, :].rearrange("a p t -> p (a t)"),
                             XN2S[:, :]).then_inc(xn2_saved, 16)

            batches(sp, one)
            save_xn2(Batch(B, 0, order=MISC_END))

            sp.wait_ge(xn2_saved, 16 * B)

            def load_xn2(b, par):
                sp.dma_start(XS[par][:, :], xn2_dram[bass.ds(b, 1), :, :].rearrange("a p t -> p (a t)")
                             ).then_inc(xs_ready[par], 16)

            def store(b, par):
                sp.wait_ge(tile_out, 4 * b + 4)
                sp.dma_start(out[bass.ds(b, 1), :, :].rearrange("b (t p) c -> p (b t) c", p=P),
                             OUTB[par][:, :, :]).then_inc(out_saved[par], 16)
            load_xn2(0, 0)
            load_xn2(1, 1)
            with sp.Fori(0, B - 3, 2) as i:
                for par in range(2):
                    store(i + par, par)
                    load_xn2(i + 2 + par, par)
            store(B - 2, 0)
            store(B - 1, 1)
            sp.wait_ge(out_saved[0], 8 * B)
            sp.wait_ge(out_saved[1], 8 * B)

        @block.tensor
        def _(pe):
            def misc(bt, name):
                n = bt.misc(name)
                if not isinstance(n, int) or n > 0:
                    pe.wait_ge(misc_free, n)

            def score_rows(b, par, s, which):
                for r in which:
                    qb, pair, h = r // 4, 2 * s + r % 4 // 2, r % 2
                    if s == 0 and r == 0:
                        pe.wait_ge(loaded[0], 96 * b + 96)
                        pe.wait_ge(loaded[1], 96 * b + 96)
                    if not isinstance(b, int) or 64 * b + 16 * s + r >= 2:
                        pe.wait_ge(row_max, 64 * b + 16 * s + r - 1)
                    n = P * (qb + 1)
                    pe.matmul(ROWP[r % 2][:, 0:n], QP[par][0:ROWS_K, pair, P * qb:n],
                              KZ[par][h][0:ROWS_K, pair, 0:n], start=True, stop=True).then_inc(rows_ready, 1)

            def chunk(bt, s, c):
                b, par = bt.b, bt.par
                if c == 0:
                    pe.wait_ge(misc_free, bt.base if s == 0 else bt.misc(f"mx{s}") + 1)
                if not isinstance(b, int) or 20 * b + 5 * s + c >= 2:
                    pe.wait_ge(exp_done, 20 * b + 5 * s + c - 1)
                bank = CH[(5 * s + c) % 2]
                if c == 2:
                    parts = [(i, 2, 256 * i) for i in range(4)]
                else:
                    i = {0: 0, 1: 1, 3: 2, 4: 3}[c]
                    parts = [(i, 0, 0), (i, 1, T), (i, 3, 2 * T - P)]
                for i, kb, col in parts:
                    pair, n = 2 * s + i // 2, T - P * kb
                    last = pe.matmul(bank[:, col:col + n], KZ[par][i % 2][0:ALL_K, pair, P * kb:P * kb + P],
                                     QP[par][0:ALL_K, pair, P * kb:T], start=True, stop=True)
                last.then_inc(chunk_ready, 1)

            def values(b, par, s, kbs):
                if kbs[0] == 0:
                    pe.wait_ge(causal_done, 20 * b + 5 * s + 5)
                    if not isinstance(b, int) or 4 * b + s > 0:
                        pe.wait_ge(pv_copied, 4 * b + s)
                for kb in kbs:
                    for i in range(4):
                        ch = (0, 1, 3, 4)[i]
                        c, col = {0: (ch, 0), 1: (ch, T), 2: (2, 256 * i), 3: (ch, 2 * T - P)}[kb]
                        v = VKB * kb + VS * (4 * s + i)
                        last = pe.matmul(PVB[32 * i:32 * i + 32, P * kb:T], VP[par][:, v:v + 32],
                                         PT[s % 2][:, c, col:col + T - P * kb],
                                         start=(kb == 0), stop=(kb == 3))
                if kbs[-1] == 3:
                    last.then_inc(pv_done, 1)

            def transposes(src):
                for t in range(TB):
                    last = pe.transpose(MB[:, P * t:P * t + P], src(t), IDF[:, :])
                return last

            def out_transposed(bt, b, s, name):
                misc(bt, name)
                pe.wait_ge(pv_copied, 4 * b + s + 1)
                transposes(lambda t: OT[:, P * t:P * t + P]).then_inc(misc_full, 1)

            def max_rows(bt, b, s):
                misc(bt, f"mx{s}")
                pe.wait_ge(nmax_ready, 4 * b + s + 1)
                for j in range(2):
                    for qb in range(TB):
                        col = T * j + P * qb
                        last = pe.transpose(MBH[MAX_ROW:MAX_ROW + 4, col:col + P],
                                            NMX[:, 2 * qb + j, :, :].rearrange("p h n -> p (h n)"), IDB[:, :])
                last.then_inc(misc_full, 1)

            def xn_transposed(bt):
                misc(bt, "xnT")
                pe.wait_ge(xn_ready, bt.b + 2)
                transposes(lambda t: XN[:, t, :]).then_inc(misc_full, 1)

            def project(bt, name, weight):
                misc(bt, name)
                pe.matmul(MB[:, :], weight, XNT[:, :], start=True, stop=True).then_inc(misc_full, 1)

            def q(bt): project(bt, "q", WQKV[:, 0:C])
            def qs(bt): project(bt, "qs", WSWAP[:, 0:C])
            def k(bt): project(bt, "k", WQKV[:, C:2 * C])
            def ks(bt): project(bt, "ks", WSWAP[:, C:2 * C])

            def by_tiles(bt, name, src, weight, n):
                misc(bt, name)
                for t in range(TB):
                    last = pe.matmul(MB[:, n * t:n * t + n], src[:, P * t:P * t + P], weight,
                                     start=True, stop=True)
                last.then_inc(misc_full, 1)

            def v(bt): by_tiles(bt, "v", XNT, WQKV[:, 2 * C:3 * C], C)
            def y_transposed(bt):
                misc(bt, "yT")
                transposes(lambda t: Y[:, t, :]).then_inc(misc_full, 1)
            def proj(bt): by_tiles(bt, "proj", YT, WPROJ[:, :], C)
            def xn2_transposed(bt):
                misc(bt, "xn2T")
                pe.wait_ge(xn2_ready, bt.b)
                transposes(lambda t: XN2[:, t, :]).then_inc(misc_full, 1)
            def logits(bt): by_tiles(bt, "logits", XN2S, WGATE[:, :], E)

            EXTRA_N = {(0, 1): xn_transposed, (0, 2): q, (0, 3): qs, (1, 0): k, (1, 1): ks, (1, 3): v}
            EXTRA_P = {(1, 2): y_transposed, (2, 0): proj, (3, 0): xn2_transposed, (3, 2): logits}

            pe.wait_ge(ident_loaded, 16)
            pe.wait_ge(built, 8)
            start = Batch(-1, 1, order=MISC_START)
            xn_transposed(start)
            pe.wait_ge(weights, 128)
            for op in (q, qs, k, ks, v):
                op(start)
            score_rows(0, 0, 0, range(16))
            max_rows(start, 0, 0)
            pe.wait_ge(one_rows, 64)

            def one(bt):
                b, par = bt.b, bt.par
                for s in range(4):
                    nb, npar, ns = (b, par, s + 1) if s < 3 else (b + 1, 1 - par, 0)
                    vb, vpar, vs = (b, par, s - 1) if s > 0 else (b - 1, 1 - par, 3)
                    has_next, has_values = s < 3 or bt.nxt, s > 0 or bt.prev
                    for c in range(4):
                        if has_next:
                            score_rows(nb, npar, ns, range(4 * c, 4 * c + 4))
                        chunk(bt, s, c)
                        if has_values and c > 0:
                            values(vb, vpar, vs, ((0,), (1,), (2, 3))[c - 1])
                        if bt.nxt and (s, c) in EXTRA_N:
                            EXTRA_N[s, c](bt)
                        if bt.prev and (s, c) in EXTRA_P:
                            EXTRA_P[s, c](bt)
                    chunk(bt, s, 4)
                    if has_values:
                        out_transposed(bt, vb, vs, f"ot{vs}")
                    if has_next:
                        max_rows(bt, nb, ns)

            batches(pe, one)
            end = Batch(B, 0, order=MISC_END)
            values(B - 1, 1, 3, (0, 1, 2, 3))
            out_transposed(end, B - 1, 3, "ot3")
            y_transposed(end)
            proj(end)
            xn2_transposed(end)
            logits(end)

            with pe.Fori(0, SINKHORN_ITERS) as i:
                pe.wait_ge(sink_prod, i + 1)
                for t in range(TB):
                    last = pe.matmul(MB[:, 0:B * E], ONES[:, :], PROD[:, t, :, :].rearrange("p b e -> p (b e)"),
                                     start=(t == 0), stop=(t == TB - 1))
                last.then_inc(sink_sum, 1)
            pe.wait_ge(sink_prod, SINKHORN_ITERS + 1)
            for t in range(TB):
                last = pe.transpose(PVB[0:B * E, P * t:P * t + P], PROD[:, t, :, :].rearrange("p b e -> p (b e)"), IDF[:, :])
            last.then_inc(gt_ready, 1)
            pe.wait_ge(topi_ready, 1)
            pe.transpose(MB[:, 0:B * E], TOPF[:, :, :].rearrange("p a j -> p (a j)"),
                         IDF[0:B * E, 0:B * E]).then_inc(it_ready, 1)
            pe.sem_inc(onehot_used, 2)
            with pe.Fori(0, B) as b:
                for e2 in range(E // 2):
                    pe.wait_ge(onehot, 4 * b + e2 + 1)
                    for t in range(TB):
                        last = pe.matmul(ROWP[0][:, bass.ds(32 * b + (8 * t + 2 * e2), 2)],
                                         OH[e2 % 2][:, P * t:P * t + P], RANKC[:, :], start=True, stop=True)
                    last.then_inc(onehot_used, 1)
            def tiles(b, par):
                pe.wait_ge(xs_ready[par], 8 * (b - par) + 16)
                for t in range(TB):
                    if not isinstance(b, int) or b > 0 or t >= 2:
                        pe.wait_ge(pa_ready, 4 * b + t - 1)
                        pe.wait_ge(lower, 4 * b + t - 1)
                    for half in range(2):
                        last = pe.matmul(CH[t % 2][:, T * half:T * half + T], XS[par][:, P * t:P * t + P],
                                         WEXP[:, 4 * half:4 * half + 4, :].rearrange("p e o -> p (e o)"),
                                         start=True, stop=True)
                    last.then_inc(y_full, 1)
            tiles(0, 0)
            tiles(1, 1)
            with pe.Fori(2, B - 1, 2) as i:
                tiles(i, 0)
                tiles(i + 1, 1)

        @block.scalar
        def _(act):
            def take(bt, name, dst, src):
                act.wait_ge(misc_full, bt.misc(name) + 1)
                act.activation(dst, src, ACT.Copy).then_inc(misc_free, 1)

            def xn_taken(bt): take(bt, "xnT", XNT[:, :], MB[:, :])
            def v_taken(bt):
                dst = VP[1 - bt.par][:, :].rearrange("p (t v) -> p t v", t=TB)[:, :, 0:H * VS]
                for t in range(TB):
                    if t == 0:
                        act.wait_ge(misc_full, bt.misc("v") + 1)
                    last = act.activation(dst[:, t].rearrange("p (h d) -> p h d", d=VS)[:, :, 0:HD],
                                          MB4[:, t].rearrange("p (h d) -> p h d", d=HD), ACT.Copy)
                last.then_inc(misc_free, 1)
            def y_taken(bt): take(bt, "yT", YT[:, :], MB[:, :])
            def xn2_taken(bt):
                if not isinstance(bt.b, int) or bt.b > 1:
                    act.wait_ge(xn2_saved, 16 * bt.b - 16)
                take(bt, "xn2T", XN2S[:, :], MB[:, :])

            def cut(b, w, i):
                act.wait_ge(resid[w], 3 * b + i + 1)
                if i == 0 and not (isinstance(b, int) and b == 0):
                    act.wait_ge(stored[w], 32 * b)
                act.activation(PARTS[w][:, i, :], RES[w][:, :], ACT.Copy).then_inc(part[w], 1)

            def exps(b, s, c):
                act.wait_ge(chunk_ready, 20 * b + 5 * s + c + 1)
                if c == 0 and not (isinstance(b, int) and 4 * b + s < 2):
                    act.wait_ge(pv_done, 4 * b + s - 1)
                act.activation(PT[s % 2][:, c, :], CH[(5 * s + c) % 2][:, :], ACT.Exp).then_inc(exp_done, 1)

            def values_taken(b, s):
                act.wait_ge(pv_done, 4 * b + s + 1)
                act.activation(OT[:, :], PVB[:, :], ACT.Copy).then_inc(pv_copied, 1)

            CUTS = {(1, 0): [(0, 0)], (1, 2): [(0, 1)], (1, 4): [(0, 2), (1, 0)], (2, 1): [(1, 1)], (2, 3): [(1, 2)]}
            EXTRA_N = {(0, 1): xn_taken, (1, 3): v_taken}
            EXTRA_P = {(1, 2): y_taken, (3, 0): xn2_taken}

            start = Batch(-1, 1, order=MISC_START)
            xn_taken(start)
            for w in range(2):
                for i in range(3):
                    cut(0, w, i)
            act.wait_ge(built, 8)
            v_taken(start)

            def one(bt):
                for s in range(4):
                    vb, vs = (bt.b, s - 1) if s > 0 else (bt.b - 1, 3)
                    for c in range(5):
                        exps(bt.b, s, c)
                        if c == 3 and (s > 0 or bt.prev):
                            values_taken(vb, vs)
                        if bt.nxt and (s, c) in EXTRA_N:
                            EXTRA_N[s, c](bt)
                        if bt.prev and (s, c) in EXTRA_P:
                            EXTRA_P[s, c](bt)
                        if bt.nxt:
                            for w, i in CUTS.get((s, c), ()):
                                cut(bt.b + 1, w, i)

            batches(act, one)
            end = Batch(B, 0, order=MISC_END)
            values_taken(B - 1, 3)
            y_taken(end)
            xn2_taken(end)

            act.wait_ge(w_ready, 1)

            def weigh(b):
                for t in range(TB):
                    act.wait_ge(y_full, 4 * b + t + 1)
                    if not isinstance(b, int) or b > 0 or t >= 2:
                        act.wait_ge(lower, 4 * b + t - 1)
                    for e in range(4):
                        last = act.activation(PA[t % 2][:, e, :], CH[t % 2][:, T + C * e:T + C * e + C], ACT.Copy,
                                              scale=W[:, bass.ds(32 * b + (8 * t + 4 + e), 1)])
                    last.then_inc(pa_ready, 1)
            weigh(0)
            with act.Fori(1, B) as b:
                weigh(b)

        @block.gpsimd
        def _(pool):
            pool.memset(NHALF[:, :], -0.5)
            pool.memset(ONES[:, :], 1.0).then_inc(built, 1)
            pool.memset(ONER[:, :], 1.0).then_inc(built, 1)
            for i in range(2):
                pool.memset(KZ[i][1][:, :, :].rearrange("p a t -> p (a t)").bitcast(U32), 0).then_inc(built, 1)

            def rstd(b, stats, mv, dst, done):
                pool.wait_ge(stats, b + 1)
                pool.nop(nofuse=True)
                pool.tensor_scalar(dst[:, :], mv[:, :, 1], LN_EPS, None, ALU.add)
                pool.drain()
                pool.tensor_tensor(dst[:, :], dst[:, :], NHALF[:, :], ALU.pow).then_inc(done, 1)

            def rotate(bt, w):
                b = bt.b + 1
                pool.wait_ge(misc_free, bt.misc(("qs", "ks")[w]) + 1)
                if not (isinstance(b, int) and b == 0):
                    pool.wait_ge(part[w], 3 * b)
                pool.tensor_tensor(RES[w][:, :], TC[:, :], TS[:, :], ALU.add).then_inc(resid[w], 1)

            def subtract(b, w, i):
                pool.wait_ge(part[w], 3 * b + i + 1)
                pool.tensor_tensor(RES[w][:, :], RES[w][:, :], PARTS[w][:, i, :], ALU.subtract).then_inc(resid[w], 1)

            def causal(b, s, c):
                pool.wait_ge(exp_done, 20 * b + 5 * s + c + 1)
                pool.nop(nofuse=True)
                p = PT[s % 2][:, c, :]
                if c == 2:
                    views = [(p.rearrange("p (i t) -> p i t", i=4)[:, :, 0:P], 4)]
                else:
                    views = [(p.rearrange("p (i t) -> p i t", i=2)[:, :, 0:P], 2), (p[:, 2 * T - P:2 * T], 1)]
                for v, n in views:
                    pattern = [[0, n], [1, P]] if n > 1 else [[1, P]]
                    last = pool.affine_select(out=v, in_=v, pattern=pattern, compare_op=ALU.is_ge, fill=0.0,
                                              base=0, channel_multiplier=-1)
                last.then_inc(causal_done, 1)

            rstd(0, ln_stats, MV, RSTD, ln_rstd)
            start = Batch(-1, 1, order=MISC_START)
            for w in range(2):
                rotate(start, w)
                subtract(0, w, 0)
                subtract(0, w, 1)

            NEXT_OPS = {(0, 0): [lambda bt: rstd(bt.b + 1, ln_stats, MV, RSTD, ln_rstd)],
                        (0, 4): [lambda bt: rotate(bt, 0)],
                        (1, 1): [lambda bt: subtract(bt.b + 1, 0, 0)],
                        (1, 3): [lambda bt: subtract(bt.b + 1, 0, 1), lambda bt: rotate(bt, 1)],
                        (2, 0): [lambda bt: subtract(bt.b + 1, 1, 0)],
                        (2, 2): [lambda bt: subtract(bt.b + 1, 1, 1)]}

            def one(bt):
                for s in range(4):
                    for c in range(5):
                        causal(bt.b, s, c)
                        if bt.nxt:
                            for op in NEXT_OPS.get((s, c), ()):
                                op(bt)
                        if bt.prev and (s, c) == (2, 2):
                            rstd(bt.b - 1, ln2_stats, MV2, RSTD2, ln2_rstd)

            batches(pool, one)
            rstd(B - 1, ln2_stats, MV2, RSTD2, ln2_rstd)

            def finish(b, par):
                if not isinstance(b, int) or b >= 2:
                    pool.wait_ge(out_saved[par], 8 * (b - par))
                for t in range(TB):
                    pool.wait_ge(lower, 4 * b + t + 1)
                    pool.tensor_tensor(O1[t % 2][:, :], S2[t % 2][:, 0, :], S2[t % 2][:, 1, :], ALU.add)
                    pool.drain()
                    pool.tensor_tensor(OUTB[par][:, t, :], O1[t % 2][:, :],
                                       X[:, bass.ds(4 * b + t, 1), :].rearrange("p a c -> p (a c)"),
                                       ALU.add).then_inc(tile_out, 1)
            finish(0, 0)
            finish(1, 1)
            with pool.Fori(2, B - 1, 2) as i:
                finish(i, 0)
                finish(i + 1, 1)

        @block.vector
        def _(dve):
            dve.memset(KZ[0][0][:, :, :].rearrange("p a t -> p (a t)").bitcast(U32), 0).then_inc(built, 1)
            dve.memset(KZ[1][0][:, :, :].rearrange("p a t -> p (a t)").bitcast(U32), 0).then_inc(built, 1)

            def tile_of(b, t):
                return X[:, bass.ds(4 * b + t, 1), :].rearrange("p a c -> p (a c)")

            def statistics(b, st, mv, done):
                for t in range(TB):
                    dve.bn_stats(out=st[:, t, :], in_=tile_of(b, t))
                dve.drain()
                for t in range(TB):
                    last = dve.bn_aggr(out=mv[:, t, :], in_=st[:, t, :])
                last.then_inc(done, 1)

            def normalize(b, mv, rs, got, dst, done):
                dve.wait_ge(got, b + 1)
                for t in range(TB):
                    last = dve.tensor_scalar(dst[:, t, :], tile_of(b, t), mv[:, t, 0:1], rs[:, t:t + 1],
                                             ALU.subtract, ALU.mult)
                last.then_inc(done, 1)

            def turn(bt, name, i, w, dst):
                b = bt.b + 1
                if i % 2 == 0:
                    if w == 1:
                        dve.wait_ge(resid[0], 3 * b + 1)
                    elif not (isinstance(b, int) and b == 0):
                        dve.wait_ge(resid[1], 3 * b - 2)
                dve.wait_ge(misc_full, bt.misc(name) + 1)
                dve.tensor_tensor(dst[:, :], MB[:, :], ROPE[:, i, :], ALU.mult).then_inc(misc_free, 1)

            def row_maxima(b, s, which):
                for r in which:
                    n = P * (r // 4 + 1)
                    dve.wait_ge(rows_ready, 64 * b + 16 * s + r + 1)
                    dve.nop(nofuse=True)
                    dve.tensor_tensor_reduce(out=JUNK[r % 2][:, 0:n], in0=ROWP[r % 2][:, 0:n], in1=TRI[:, T - n:T],
                                             scale=1.0, scalar=-3e38, op0=ALU.add, op1=ALU.max,
                                             accum_out=MX[s % 2][:, r:r + 1]).then_inc(row_max, 1)

            def minus_max(s):
                mx = MX[s % 2][:, :].rearrange("p (a h) -> p a h", h=2)
                dve.drain()
                dve.tensor_scalar(NMX[:, :, :, 0], mx, -1.0, None, ALU.mult)
                dve.drain()
                dve.scalar_tensor_tensor(out=NMX[:, :, :, 1], in0=mx, scalar=-1.0, in1=NMX[:, :, :, 0],
                                         op0=ALU.mult, op1=ALU.subtract).then_inc(nmax_ready, 1)

            def max_rows_taken(bt, par, s):
                dve.wait_ge(misc_full, bt.misc(f"mx{s}") + 1)
                dve.tensor_copy(QP[par][MAX_ROW:MAX_ROW + 4, 2 * s:2 * s + 2, :].rearrange("p a t -> p (a t)"),
                                MBH[MAX_ROW:MAX_ROW + 4, :]).then_inc(misc_free, 1)

            def out_taken(bt, s):
                o = MB[:, :].rearrange("p (t i r) -> p t i r", t=TB, i=4)
                y = Y[:, :, 32 * s:32 * s + 32].rearrange("p t (i d) -> p t i d", i=4)
                dve.wait_ge(misc_full, bt.misc(f"ot{s}") + 1)
                dve.reciprocal(RSUM[:, :, :], o[:, :, :, HD])
                dve.drain()
                dve.tensor_tensor(y, o[:, :, :, 0:HD], RSUM[:, :, :].unsqueeze(3).to_broadcast([P, TB, 4, HD]),
                                  ALU.mult).then_inc(misc_free, 1)

            def add_attention(bt):
                dve.wait_ge(misc_full, bt.misc("proj") + 1)
                xt = X[:, bass.ds(4 * (bt.b - 1), TB), :].rearrange("p t c -> p (t c)")
                dve.tensor_tensor(xt, MB[:, :], xt, ALU.add).then_inc(misc_free, 1)
                dve.drain()
                statistics(bt.b - 1, ST2, MV2, ln2_stats)

            def clip_logits(bt):
                dve.wait_ge(misc_full, bt.misc("logits") + 1)
                dve.tensor_scalar(LG[:, bass.ds(4 * (bt.b - 1), TB), :].rearrange("p t e -> p (t e)"),
                                  MB[:, 0:TB * E], CLIP_EPS, None, ALU.max).then_inc(misc_free, 1)

            EXTRA_N = {(0, 0): lambda bt: statistics(bt.b + 1, ST, MV, ln_stats),
                       (0, 2): lambda bt: turn(bt, "q", 0, 0, TC), (0, 3): lambda bt: turn(bt, "qs", 1, 0, TS),
                       (1, 0): lambda bt: turn(bt, "k", 2, 1, TC), (1, 1): lambda bt: turn(bt, "ks", 3, 1, TS)}
            EXTRA_P = {(2, 0): add_attention, (3, 2): clip_logits}

            dve.wait_ge(x_first, 16)
            statistics(0, ST, MV, ln_stats)
            normalize(0, MV, RSTD, ln_rstd, XN, xn_ready)
            for i in range(2):
                dve.memset(VP[i][:, :], 1.0).then_inc(built, 1)
            dve.wait_ge(ident_loaded, 16)
            dve.wait_ge(weights, 128)
            dve.tensor_copy(IDB[:, :], IDF[:, :])
            dve.tensor_copy(RANKC[:, :], SMALL[:, T:T + 2])
            dve.drain()
            start = Batch(-1, 1, order=MISC_START)
            turn(start, "q", 0, 0, TC)
            turn(start, "qs", 1, 0, TS)
            turn(start, "k", 2, 1, TC)
            turn(start, "ks", 3, 1, TS)
            row_maxima(0, 0, range(16))
            minus_max(0)
            max_rows_taken(start, 0, 0)
            dve.wait_ge(x_rest, 16 * (B - 1))

            def one(bt):
                b, par = bt.b, bt.par
                for s in range(4):
                    nb, npar, ns = (b, par, s + 1) if s < 3 else (b + 1, 1 - par, 0)
                    has_next, has_values = s < 3 or bt.nxt, s > 0 or bt.prev
                    for c in range(4):
                        if has_next:
                            row_maxima(nb, ns, range(4 * c, 4 * c + 4))
                        if bt.nxt and (s, c) in EXTRA_N:
                            EXTRA_N[s, c](bt)
                        if bt.prev and (s, c) in EXTRA_P:
                            EXTRA_P[s, c](bt)
                        if c == 0 and s == 0 and bt.nxt:
                            normalize(b + 1, MV, RSTD, ln_rstd, XN, xn_ready)
                        if c == 3 and s == 2 and bt.prev:
                            normalize(b - 1, MV2, RSTD2, ln2_rstd, XN2, xn2_ready)
                    if has_next:
                        minus_max(ns)
                    if has_values:
                        out_taken(bt, (s - 1) % 4)
                    if has_next:
                        max_rows_taken(bt, npar, ns)

            batches(dve, one)
            end = Batch(B, 0, order=MISC_END)
            out_taken(end, 3)
            add_attention(end)
            normalize(B - 1, MV2, RSTD2, ln2_rstd, XN2, xn2_ready)
            clip_logits(end)
            dve.drain()

            def per_token(v):
                return v[:, :].rearrange("p (b t) -> p b t", b=B).unsqueeze(3).to_broadcast([P, B, TB, E])
            prod4 = PROD[:, :, :, :].rearrange("p t b e -> p b t e")
            lg4 = LG[:, :, :].rearrange("p (b t) e -> p b t e", b=B)
            dve.tensor_reduce(out=RSC[:, :], in_=LG[:, :, :], axis=AX.X, op=ALU.max)
            dve.drain()
            dve.reciprocal(RINV[:, :], RSC[:, :])
            dve.drain()
            dve.tensor_tensor(KT[:, :, :, :], lg4, per_token(RINV), ALU.mult)
            dve.drain()
            dve.tensor_tensor(prod4, KT[:, :, :, :], per_token(RSC), ALU.mult).then_inc(sink_prod, 1)

            def rescale(i):
                dve.wait_ge(sink_sum, i + 1)
                dve.reciprocal(CSC[:, :, :].rearrange("p b e -> p (b e)"), MB[:, 0:B * E])
                dve.drain()
                dve.tensor_tensor(SCALED[:, :, :, :], KT[:, :, :, :],
                                  CSC[:, :, :].unsqueeze(2).to_broadcast([P, B, TB, E]), ALU.mult)
                dve.drain()
                dve.tensor_reduce(out=RINV[:, :], in_=SCALED[:, :, :, :].rearrange("p b t e -> p (b t) e"),
                                  axis=AX.X, op=ALU.add)
                dve.drain()
                dve.reciprocal(RSC[:, :], RINV[:, :])
                dve.drain()

            with dve.Fori(0, SINKHORN_ITERS - 1) as i:
                rescale(i)
                dve.tensor_tensor(prod4, KT[:, :, :, :], per_token(RSC), ALU.mult).then_inc(sink_prod, 1)
            rescale(SINKHORN_ITERS - 1)
            dve.tensor_tensor(prod4, SCALED[:, :, :, :], per_token(RSC), ALU.mult).then_inc(sink_prod, 1)

            dve.wait_ge(gt_ready, 1)
            dve.tensor_copy(GT[:, :], PVB[0:B * E, :])
            dve.drain()
            with dve.Fori(0, TOPK - 8, 8) as r:
                dve.max(out=TOPV[:, :], in_=GT[:, :])
                dve.drain()
                dve.max_index(out=TOPI8[:, :], in_max=TOPV[:, :], in_values=GT[:, :])
                dve.match_replace(out=GT[:, :], in_to_replace=TOPV[:, :], in_values=GT[:, :], imm_value=-1.0)
                dve.drain()
                dve.tensor_copy(TOPF[:, 0, bass.ds(r, 8)], TOPI8[:, :])
                dve.tensor_copy(TOPF[:, 1, bass.ds(r, 8)], TOPI8[:, :])
            dve.max(out=TOPV[:, :], in_=GT[:, :])
            dve.drain()
            dve.max_index(out=TOPI8[:, :], in_max=TOPV[:, :], in_values=GT[:, :])
            dve.drain()
            dve.tensor_copy(TOPF[:, 0, TOPK - 8:TOPK], TOPI8[:, :])
            dve.tensor_copy(TOPF[:, 1, TOPK - 8:TOPK], TOPI8[:, :]).then_inc(topi_ready, 1)
            dve.wait_ge(it_ready, 1)
            for half in range(2):
                dve.tensor_copy(IT[64 * half:64 * half + 64, :],
                                MB[64 * half:64 * half + 64, 0:B * E].rearrange("p (c h) -> p c h", h=2)[:, :, half])
            dve.drain()
            with dve.Fori(0, B) as b:
                for e2 in range(E // 2):
                    dve.wait_ge(onehot_used, 4 * b + e2 + 1)
                    dve.tensor_scalar(OH[e2 % 2][:, :], SMALL[:, 0:T], IT[:, bass.ds(4 * b + e2, 1)], None,
                                      ALU.is_equal).then_inc(onehot, 1)

            dve.wait_ge(onehot_used, 2 + 4 * B)
            numbers = SMALL[:, T + 2:T + 2 + E].unsqueeze(1).to_broadcast([P, B * TB, E])
            dve.scalar_tensor_tensor(out=KEY[:, :, :], in0=ROWP[0][:, 0:B * TB * E].rearrange("p (t e) -> p t e", e=E),
                                     scalar=float(E), in1=numbers, op0=ALU.mult, op1=ALU.add)
            dve.drain()
            dve.tensor_reduce(out=KMAX[:, :], in_=KEY[:, :, :], axis=AX.X, op=ALU.max)
            dve.drain()
            dve.tensor_tensor(HARD[:, :, :], KEY[:, :, :], KMAX[:, :].unsqueeze(2).to_broadcast([P, B * TB, E]),
                              ALU.is_equal)
            dve.drain()
            dve.scalar_tensor_tensor(out=HARD[:, :, :], in0=KEY[:, :, :], scalar=float(E), in1=HARD[:, :, :],
                                     op0=ALU.is_ge, op1=ALU.mult)
            dve.drain()
            dve.tensor_scalar(SCALED[:, :, :, :], prod4, 0.5, None, ALU.is_gt)
            dve.drain()
            dve.tensor_tensor(W[:, :], HARD[:, :, :].rearrange("p t e -> p (t e)"),
                              SCALED[:, :, :, :].rearrange("p b t e -> p (b t e)"), ALU.mult).then_inc(w_ready, 1)
            dve.drain()

            def add_lower(b):
                for t in range(TB):
                    dve.wait_ge(y_full, 4 * b + t + 1)
                    dve.wait_ge(pa_ready, 4 * b + t + 1)
                    for e in range(4):
                        dve.scalar_tensor_tensor(out=SS[t % 2][:, e, :], in0=CH[t % 2][:, C * e:C * e + C],
                                                 scalar=W[:, bass.ds(32 * b + (8 * t + e), 1)],
                                                 in1=PA[t % 2][:, e, :], op0=ALU.mult, op1=ALU.add)
                    dve.drain()
                    if not isinstance(b, int) or b > 0 or t >= 2:
                        dve.wait_ge(tile_out, 4 * b + t - 1)
                    dve.tensor_tensor(S2[t % 2][:, :, :], SS[t % 2][:, 0:2, :], SS[t % 2][:, 2:4, :], ALU.add).then_inc(lower, 1)
            add_lower(0)
            with dve.Fori(1, B) as b:
                add_lower(b)


_OUT = (B, T, C)


def _layout():
    half, d, pair = np.meshgrid(np.arange(2), np.arange(HD), np.arange(PAIRS), indexing="ij")
    cols = ((2 * pair + half) * HD + d).reshape(-1)
    swap = ((2 * pair + half) * HD + (d ^ 1)).reshape(-1)
    inv = (np.float32(1.0) / np.float32(10000.0) ** (np.arange(0, HD, 2, dtype=np.float32) / np.float32(HD)))
    freqs = np.arange(T, dtype=np.float32)[:, None] * inv.astype(np.float32)[None, :]
    cos, sin = np.cos(freqs).astype(np.float32), np.sin(freqs).astype(np.float32)
    dd = d.reshape(-1)
    c = cos[:, dd // 2].T
    s = sin[:, dd // 2].T * np.where(dd % 2 == 0, -1.0, 1.0)[:, None].astype(np.float32)
    scale = np.float32(1.0) / np.sqrt(np.float32(HD))
    rope = np.stack([c * scale, s * scale, c, s], axis=1).astype(np.float32)
    tri = np.zeros((P, T), np.float32)
    q, k = np.meshgrid(np.arange(P), np.arange(P), indexing="ij")
    tri[:, T - P:] = np.where(k > q, np.float32(-3e38), np.float32(0))
    small = np.zeros((P, T + 2 + E), np.float32)
    small[:, 0:T] = np.arange(T)
    place = np.arange(P) % TOPK + 1
    small[:, T] = np.where(np.arange(P) < TOPK, place, 0)
    small[:, T + 1] = np.where(np.arange(P) >= TOPK, place, 0)
    small[:, T + 2:] = np.arange(E)
    return cols, swap, rope, tri, small


def kernel(L0_attn_x, L0_attn_W_attn, L0_attn_W_proj, L0_ffn_gate_w, L0_ffn_experts):
    import concourse.bacc as _bacc
    from concourse.bass_utils import run_bass_kernel_spmd as _run

    cols, swap, rope, tri, small = _layout()
    w = np.asarray(L0_attn_W_attn)
    arrays = {
        "x": np.ascontiguousarray(L0_attn_x),
        "w_qkv": np.ascontiguousarray(np.concatenate([w[:, cols], w[:, C + cols], w[:, 2 * C:]], axis=1)),
        "w_swap": np.ascontiguousarray(np.concatenate([w[:, swap], w[:, C + swap]], axis=1)),
        "w_proj": np.ascontiguousarray(L0_attn_W_proj),
        "gate_w": np.ascontiguousarray(np.asarray(L0_ffn_gate_w)[0]),
        "experts": np.ascontiguousarray(L0_ffn_experts),
        "rope": rope, "tri": tri, "ident": np.eye(P, dtype=np.float32), "small": small,
    }
    nc = _bacc.Bacc("TRN2", target_bir_lowering=False, num_devices=1)
    args = [nc.dram_tensor(f"in_{name}", a.shape, mybir.dt.from_np(a.dtype), kind="ExternalInput").ap()
            for name, a in arrays.items()]
    out = nc.dram_tensor("out_0", _OUT, F32, kind="ExternalOutput").ap()
    build(nc, *args, out)
    r = _run(nc, [{f"in_{name}": a for name, a in arrays.items()}], core_ids=[0])
    return r.results[0]["out_0"]
```

```python
import numpy as np
import concourse.bass as bass
from concourse import mybir
from contextlib import ExitStack

F32 = mybir.dt.float32
BF16 = mybir.dt.bfloat16
U32 = mybir.dt.uint32
ACT = mybir.ActivationFunctionType
ALU = mybir.AluOpType
AX = mybir.AxisListType

B, T, C = 8, 512, 128
H, HD = 16, 8
E = 8
P = 128
TB = T // P
PAIRS = H // 2
TOPK = T // E
SINKHORN_ITERS = 8
LN_EPS = 1e-5
CLIP_EPS = 1e-6

Q_PART = [0, 0, 0, 1, 1, 2]
K_PART = [0, 1, 2, 0, 1, 0]
HEAD_ROWS = len(Q_PART) * HD
ROWS_K = 2 * HEAD_ROWS
MAX_ROW = ROWS_K
ALL_K = MAX_ROW + 4
VS = HD + 1
VKB = H * VS + 32

STEP = [("u", 0), ("c", 0), ("u", 1), ("v", 0), ("x", 0), ("u", 2), ("c", 1), ("u", 3), ("x", 1),
        ("u", 4), ("c", 2), ("u", 5), ("v", 1), ("x", 2), ("u", 6), ("c", 3), ("u", 7), ("x", 3),
        ("u", 8), ("v", 2), ("u", 9), ("c", 4), ("x", 4)]
EXTRAS = {(0, 1): "xnT n", (0, 2): "q n", (0, 3): "qs n", (0, 4): "k n",
          (1, 0): "ks n", (1, 2): "v n", (1, 3): "yT p",
          (2, 1): "proj p", (3, 0): "xn2T p", (3, 2): "logits p"}
UNITS = [[(3, i, 0)] for i in range(4)] + [[(2, i, 0), (0, i, 3 * P)] for i in range(4)] + \
        [[(1, 2 * i, 0), (1, 2 * i + 1, 2 * P)] for i in range(2)]
NU = len(UNITS)
NC = 5


def _shared_bank_order():
    order = []
    for s in range(4):
        order += [EXTRAS[s, x] for x in range(5) if (s, x) in EXTRAS]
        order += [f"ot{s - 1}" if s > 0 else "ot3 p", f"mx{s + 1}" if s < 3 else "mx0 n"]
    return order


MISC = _shared_bank_order()
MISC_START = ["xnT n", "q n", "qs n", "k n", "ks n", "v n", "mx0 n"]
MISC_END = ["ot3 p", "yT p", "proj p", "xn2T p", "logits p"]
PREV = sum(m.endswith("p") for m in MISC)
NEXT = sum(m.endswith("n") for m in MISC)


class Batch:

    def __init__(self, b, par, prev=True, nxt=True, order=MISC):
        self.b, self.par, self.prev, self.nxt = b, par, prev, nxt
        self.order = [m.split()[0] for m in order
                      if (prev or not m.endswith("p")) and (nxt or not m.endswith("n"))]
        if order is MISC_START:
            self.base = 0
        elif order is MISC_END:
            self.base = b * len(MISC) + len(MISC_START) - PREV - NEXT
        elif not prev:
            self.base = len(MISC_START)
        else:
            self.base = b * len(MISC) + (len(MISC_START) - PREV)

    def extra(self, s, x):
        name, _, kind = EXTRAS.get((s, x), "").partition(" ")
        return name if (kind == "n" and self.nxt) or (kind == "p" and self.prev) else None

    def misc(self, name):
        return self.base + self.order.index(name)


def build(nc, x_in, w_qkv, w_swap, w_proj, gate_w, experts, rope, tri, ident, small, out):
    ctx = ExitStack()
    with ctx:
        def sb(name, shape, dt=F32):
            return ctx.enter_context(nc.sbuf_tensor(name, shape, dt))

        def sem(name):
            return ctx.enter_context(nc.semaphore(name))

        WQKV = sb("WQKV", [P, 3 * C])
        WSWAP = sb("WSWAP", [P, 2 * C])
        WPROJ = sb("WPROJ", [P, C])
        WGATE = sb("WGATE", [P, E])
        WEXP = sb("WEXP", [P, E, C])
        ROPE = sb("ROPE", [P, 4, T])
        TRI = sb("TRI", [P, T])
        IDF = sb("IDF", [P, P])
        IDB = sb("IDB", [P, P], BF16)
        SMALL = sb("SMALL", [P, T + 2 + E])
        RANKC = sb("RANKC", [P, 2], BF16)
        ONES = sb("ONES", [P, P])
        NHALF = sb("NHALF", [P, B * TB])
        ONER = sb("ONER", [2, PAIRS * T], BF16)
        X = sb("X", [P, B * TB, C])
        LG = sb("LG", [P, B * TB, E])
        QP = [sb(f"QP{i}", [P, PAIRS, T], BF16) for i in range(2)]
        KZ = [[sb(f"KZ{i}{h}", [P, PAIRS, T], BF16) for h in range(2)] for i in range(2)]
        VP = [sb(f"VP{i}", [P, TB * VKB]) for i in range(2)]
        PT = [sb(f"PT{i}", [P, 5, 2 * T]) for i in range(2)]
        XN = sb("XN", [P, TB, C])
        XNT = sb("XNT", [P, T])
        ST = sb("ST", [P, B * TB, 6])
        MV = sb("MV", [P, B * TB, 2])
        RSTD = sb("RSTD", [P, B * TB])
        TC = sb("TC", [P, T])
        TS = sb("TS", [P, T])
        RES = [sb(f"RES{w}", [P, T]) for w in range(2)]
        PARTS = [sb(f"PARTS{w}", [P, 3, T], BF16) for w in range(2)]
        MX = [sb(f"MX{i}", [P, 16]) for i in range(2)]
        NMX = sb("NMX", [P, 8, 2, 2], BF16)
        JUNK = [sb(f"JUNK{i}", [P, T], BF16) for i in range(2)]
        OT = sb("OT", [P, T])
        RSUM = sb("RSUM", [P, TB, 4])
        Y = sb("Y", [P, TB, C])
        YT = sb("YT", [P, T])
        XN2 = sb("XN2", [P, TB, C])
        ST2 = sb("ST2", [P, TB, 6])
        MV2 = sb("MV2", [P, TB, 2])
        RSTD2 = sb("RSTD2", [P, TB])
        XN2S = sb("XN2S", [P, T])
        KT = sb("KT", [P, B, TB, E])
        PROD = sb("PROD", [P, TB, B, E])
        SCALED = sb("SCALED", [P, B, TB, E])
        RINV = sb("RINV", [P, B * TB])
        RSC = sb("RSC", [P, B * TB])
        CSC = sb("CSC", [P, B, E])
        GT = sb("GT", [B * E, T])
        TOPV = sb("TOPV", [B * E, 8])
        TOPI8 = sb("TOPI8", [B * E, 8], U32)
        TOPF = sb("TOPF", [B * E, 2, TOPK])
        IT = sb("IT", [P, B * E // 2])
        OH = [sb(f"OH{i}", [P, T], BF16) for i in range(2)]
        KEY = sb("KEY", [P, B * TB, E])
        KMAX = sb("KMAX", [P, B * TB])
        HARD = sb("HARD", [P, B * TB, E])
        W = sb("W", [P, B * TB * E])
        XS = [sb(f"XS{i}", [P, T]) for i in range(2)]
        PA = [sb(f"PA{i}", [P, 4, C]) for i in range(2)]
        SS = [sb(f"SS{i}", [P, 4, C]) for i in range(2)]
        S2 = [sb(f"S2{i}", [P, 2, C]) for i in range(2)]
        O1 = [sb(f"O1{i}", [P, C]) for i in range(2)]
        OUTB = [sb(f"OUTB{i}", [P, TB, C]) for i in range(2)]

        CH = [ctx.enter_context(nc.psum_tensor(f"CH{i}", [P, 2 * T], F32)) for i in range(2)]
        ROWP = [ctx.enter_context(nc.psum_tensor(f"ROWP{i}", [P, T], F32)) for i in range(2)]
        PVB = ctx.enter_context(nc.psum_tensor("PVB", [P, T], F32))
        MB = ctx.enter_context(nc.psum_tensor("MB", [P, T], F32))
        MBH = MB[:, :].bitcast(BF16)
        MB4 = MB[:, :].rearrange("p (a c) -> p a c", a=TB)

        xn2_dram = nc.dram_tensor("xn2_scratch", [B, P, T], F32, kind="Internal").ap()
        scratch = nc.dram_tensor("parts_scratch", [2, 2, 2, 3, HD, PAIRS, T], BF16, kind="Internal").ap()

        ident_loaded = sem("ident_loaded")
        x_first = sem("x_first_loaded")
        x_rest = sem("x_rest_loaded")
        weights = sem("weights_loaded")
        built = sem("constants_built")
        one_rows = sem("one_rows_loaded")
        rows_ready = sem("score_rows_ready")
        row_max = sem("row_max_done")
        nmax_ready = sem("minus_max_ready")
        chunk_ready = sem("score_chunk_ready")
        exp_done = sem("exp_done")
        causal_done = sem("causal_done")
        pv_done = sem("pv_done")
        pv_copied = sem("pv_copied")
        misc_full = sem("misc_full")
        misc_free = sem("misc_free")
        ln_stats = sem("ln_stats")
        ln_rstd = sem("ln_rstd")
        xn_ready = sem("xn_ready")
        ln2_stats = sem("ln2_stats")
        ln2_rstd = sem("ln2_rstd")
        xn2_ready = sem("xn2_ready")
        resid = [sem("q_residual"), sem("k_residual")]
        part = [sem("q_part"), sem("k_part")]
        xn2_saved = sem("xn2_saved")
        stored = [sem("q_stored"), sem("k_stored")]
        loaded = [sem("q_loaded"), sem("k_loaded")]
        sink_prod = sem("sinkhorn_product")
        sink_sum = sem("sinkhorn_sum")
        gt_ready = sem("gates_transposed")
        topi_ready = sem("top_indices")
        it_ready = sem("indices_transposed")
        onehot = sem("onehot_ready")
        onehot_used = sem("onehot_used")
        w_ready = sem("weights_of_experts")
        xs_ready = [sem("xn2_even_loaded"), sem("xn2_odd_loaded")]
        y_full = sem("expert_outputs")
        pa_ready = sem("upper_experts_weighted")
        lower = sem("lower_experts_added")
        tile_out = sem("tile_out")
        out_saved = [sem("out_even_saved"), sem("out_odd_saved")]

        block = ctx.enter_context(nc.Block())

        def batches(eng, one):
            one(Batch(0, 0, prev=False))
            with eng.Fori(1, B - 2, 2) as i:
                one(Batch(i, 1))
                one(Batch(i + 1, 0))
            one(Batch(B - 1, 1, nxt=False))

        @block.sync
        def _(sp):
            xv = x_in.rearrange("b (t p) c -> b p t c", p=P)
            Xv = [X[:, TB * b:TB * b + TB, :] for b in range(B)]
            sp.dma_start(Xv[0], xv[0]).then_inc(x_first, 16)
            sp.dma_start(IDF[:, :], ident).then_inc(ident_loaded, 16)
            sp.dma_start(WQKV[:, :], w_qkv).then_inc(weights, 16)
            sp.dma_start(WSWAP[:, :], w_swap).then_inc(weights, 16)
            sp.dma_start(ROPE[:, :, :], rope).then_inc(weights, 16)
            sp.dma_start(TRI[:, :], tri).then_inc(weights, 16)
            sp.dma_start(WPROJ[:, :], w_proj).then_inc(weights, 16)
            sp.dma_start(WGATE[:, :], gate_w).then_inc(weights, 16)
            sp.dma_start(SMALL[:, :], small).then_inc(weights, 16)
            for b in range(1, B):
                sp.dma_start(Xv[b], xv[b]).then_inc(x_rest, 16)
            sp.dma_start(WEXP[:, :, :], experts.rearrange("e d o -> d e o")).then_inc(weights, 16)
            sp.wait_ge(built, 8)
            for i in range(2):
                for h in range(2):
                    r = MAX_ROW + 2 * h
                    sp.dma_start(KZ[i][h][r:r + 2, :, :].rearrange("p a t -> p (a t)"),
                                 ONER[:, :]).then_inc(one_rows, 16)

            def trip(b, par, w, used):
                sp.wait_ge(part[w], 3 * b + 3)
                if used:
                    sp.wait_ge(chunk_ready, 20 * b - 20)
                sc = scratch[w, par]
                for h in range(2):
                    sp.dma_start(sc[h].rearrange("n d a t -> (d a) n t"),
                                 PARTS[w][64 * h:64 * h + 64, :, :]).then_inc(stored[w], 16)
                sp.wait_ge(stored[w], 32 * b + 32)
                for h in range(2):
                    rows = (QP[par] if w == 0 else KZ[par][h])[:, :, :].rearrange("p a t -> p (a t)")
                    for i, n in ((0, 3), (1, 2), (2, 1)):
                        slot = Q_PART.index(i)
                        r = HEAD_ROWS * h + HD * slot
                        if w == 0:
                            src = sc[h, i].rearrange("d a t -> d (a t)")
                            src = bass.AP(tensor=src.tensor, offset=src.offset,
                                          ap=[[0, n]] + [list(x) for x in src.ap])
                        else:
                            src = sc[h, 0:n].rearrange("n d a t -> (n d) (a t)")
                        sp.dma_start(rows[r:r + HD * n, :], src).then_inc(loaded[w], 16)

            trip(0, 0, 0, False)
            trip(0, 0, 1, False)

            def one(bt):
                if bt.nxt:
                    trip(bt.b + 1, 1 - bt.par, 0, bt.prev)
                    trip(bt.b + 1, 1 - bt.par, 1, bt.prev)
                if bt.prev:
                    save_xn2(bt)

            def save_xn2(bt):
                sp.wait_ge(misc_free, bt.misc("xn2T") + 1)
                sp.dma_start(xn2_dram[bass.ds(bt.b - 1, 1), :, :].rearrange("a p t -> p (a t)"),
                             XN2S[:, :]).then_inc(xn2_saved, 16)

            batches(sp, one)
            save_xn2(Batch(B, 0, order=MISC_END))

            sp.wait_ge(xn2_saved, 16 * B)

            def load_xn2(b, par):
                sp.dma_start(XS[par][:, :], xn2_dram[bass.ds(b, 1), :, :].rearrange("a p t -> p (a t)")
                             ).then_inc(xs_ready[par], 16)

            def store(b, par):
                sp.wait_ge(tile_out, 4 * b + 4)
                sp.dma_start(out[bass.ds(b, 1), :, :].rearrange("b (t p) c -> p (b t) c", p=P),
                             OUTB[par][:, :, :]).then_inc(out_saved[par], 16)
            load_xn2(0, 0)
            load_xn2(1, 1)
            with sp.Fori(0, B - 3, 2) as i:
                for par in range(2):
                    store(i + par, par)
                    load_xn2(i + 2 + par, par)
            store(B - 2, 0)
            store(B - 1, 1)
            sp.wait_ge(out_saved[0], 8 * B)
            sp.wait_ge(out_saved[1], 8 * B)

        @block.tensor
        def _(pe):
            def misc(bt, name):
                n = bt.misc(name)
                if not isinstance(n, int) or n > 0:
                    pe.wait_ge(misc_free, n)

            def score_rows(b, par, s, u):
                n = 4 * NU * b + NU * s + u
                if s == 0 and u == 0:
                    pe.wait_ge(loaded[0], 96 * b + 96)
                    pe.wait_ge(loaded[1], 96 * b + 96)
                if not isinstance(b, int) or n >= 2:
                    pe.wait_ge(row_max, n - 1)
                for qb, i, col in UNITS[u]:
                    pair, keys = 2 * s + i // 2, P * (qb + 1)
                    last = pe.matmul(ROWP[u % 2][:, col:col + keys], QP[par][0:ROWS_K, pair, P * qb:keys],
                                     KZ[par][i % 2][0:ROWS_K, pair, 0:keys], start=True, stop=True)
                last.then_inc(rows_ready, 1)

            def chunk(bt, s, c):
                b, par = bt.b, bt.par
                if c == 0:
                    pe.wait_ge(misc_free, bt.base if s == 0 else bt.misc(f"mx{s}") + 1)
                if not isinstance(b, int) or 20 * b + 5 * s + c >= 2:
                    pe.wait_ge(exp_done, 20 * b + 5 * s + c - 1)
                bank = CH[(5 * s + c) % 2]
                if c == 2:
                    parts = [(i, 2, 256 * i) for i in range(4)]
                else:
                    i = {0: 0, 1: 1, 3: 2, 4: 3}[c]
                    parts = [(i, 0, 0), (i, 1, T), (i, 3, 2 * T - P)]
                for i, kb, col in parts:
                    pair, n = 2 * s + i // 2, T - P * kb
                    last = pe.matmul(bank[:, col:col + n], KZ[par][i % 2][0:ALL_K, pair, P * kb:P * kb + P],
                                     QP[par][0:ALL_K, pair, P * kb:T], start=True, stop=True)
                last.then_inc(chunk_ready, 1)

            def values(b, par, s, kbs):
                if kbs[0] == 0:
                    pe.wait_ge(causal_done, 20 * b + 5 * s + 5)
                    if not isinstance(b, int) or 4 * b + s > 0:
                        pe.wait_ge(pv_copied, 4 * b + s)
                for kb in kbs:
                    for i in range(4):
                        ch = (0, 1, 3, 4)[i]
                        c, col = {0: (ch, 0), 1: (ch, T), 2: (2, 256 * i), 3: (ch, 2 * T - P)}[kb]
                        v = VKB * kb + VS * (4 * s + i)
                        last = pe.matmul(PVB[32 * i:32 * i + 32, P * kb:T], VP[par][:, v:v + 32],
                                         PT[s % 2][:, c, col:col + T - P * kb],
                                         start=(kb == 0), stop=(kb == 3))
                if kbs[-1] == 3:
                    last.then_inc(pv_done, 1)

            def transposes(src):
                for t in range(TB):
                    last = pe.transpose(MB[:, P * t:P * t + P], src(t), IDF[:, :])
                return last

            def out_transposed(bt, b, s, name):
                misc(bt, name)
                pe.wait_ge(pv_copied, 4 * b + s + 1)
                transposes(lambda t: OT[:, P * t:P * t + P]).then_inc(misc_full, 1)

            def max_rows(bt, b, s):
                misc(bt, f"mx{s}")
                pe.wait_ge(nmax_ready, 4 * b + s + 1)
                for j in range(2):
                    for qb in range(TB):
                        col = T * j + P * qb
                        last = pe.transpose(MBH[MAX_ROW:MAX_ROW + 4, col:col + P],
                                            NMX[:, 2 * qb + j, :, :].rearrange("p h n -> p (h n)"), IDB[:, :])
                last.then_inc(misc_full, 1)

            def xn_transposed(bt):
                misc(bt, "xnT")
                pe.wait_ge(xn_ready, bt.b + 2)
                transposes(lambda t: XN[:, t, :]).then_inc(misc_full, 1)

            def project(bt, name, weight):
                misc(bt, name)
                pe.matmul(MB[:, :], weight, XNT[:, :], start=True, stop=True).then_inc(misc_full, 1)

            def q(bt): project(bt, "q", WQKV[:, 0:C])
            def qs(bt): project(bt, "qs", WSWAP[:, 0:C])
            def k(bt): project(bt, "k", WQKV[:, C:2 * C])
            def ks(bt): project(bt, "ks", WSWAP[:, C:2 * C])

            def by_tiles(bt, name, src, weight, n):
                misc(bt, name)
                for t in range(TB):
                    last = pe.matmul(MB[:, n * t:n * t + n], src[:, P * t:P * t + P], weight,
                                     start=True, stop=True)
                last.then_inc(misc_full, 1)

            def v(bt): by_tiles(bt, "v", XNT, WQKV[:, 2 * C:3 * C], C)
            def y_transposed(bt):
                misc(bt, "yT")
                transposes(lambda t: Y[:, t, :]).then_inc(misc_full, 1)
            def proj(bt): by_tiles(bt, "proj", YT, WPROJ[:, :], C)
            def xn2_transposed(bt):
                misc(bt, "xn2T")
                pe.wait_ge(xn2_ready, bt.b)
                transposes(lambda t: XN2[:, t, :]).then_inc(misc_full, 1)
            def logits(bt): by_tiles(bt, "logits", XN2S, WGATE[:, :], E)

            extras = {"xnT": xn_transposed, "q": q, "qs": qs, "k": k, "ks": ks, "v": v,
                      "yT": y_transposed, "proj": proj, "xn2T": xn2_transposed, "logits": logits}

            pe.wait_ge(ident_loaded, 16)
            pe.wait_ge(built, 8)
            start = Batch(-1, 1, order=MISC_START)
            xn_transposed(start)
            pe.wait_ge(weights, 128)
            for op in (q, qs, k, ks, v):
                op(start)
            for u in range(NU):
                score_rows(0, 0, 0, u)
            max_rows(start, 0, 0)
            pe.wait_ge(one_rows, 64)

            def one(bt):
                b, par = bt.b, bt.par
                for s in range(4):
                    nb, npar, ns = (b, par, s + 1) if s < 3 else (b + 1, 1 - par, 0)
                    vb, vpar, vs = (b, par, s - 1) if s > 0 else (b - 1, 1 - par, 3)
                    has_next, has_values = s < 3 or bt.nxt, s > 0 or bt.prev
                    for kind, i in STEP:
                        if kind == "u" and has_next:
                            score_rows(nb, npar, ns, i)
                        elif kind == "c":
                            chunk(bt, s, i)
                        elif kind == "v" and has_values:
                            values(vb, vpar, vs, ((0,), (1,), (2, 3))[i])
                        elif kind == "x" and bt.extra(s, i):
                            extras[bt.extra(s, i)](bt)
                    if has_values:
                        out_transposed(bt, vb, vs, f"ot{vs}")
                    if has_next:
                        max_rows(bt, nb, ns)

            batches(pe, one)
            end = Batch(B, 0, order=MISC_END)
            values(B - 1, 1, 3, (0, 1, 2, 3))
            out_transposed(end, B - 1, 3, "ot3")
            y_transposed(end)
            proj(end)
            xn2_transposed(end)
            logits(end)

            with pe.Fori(0, SINKHORN_ITERS) as i:
                pe.wait_ge(sink_prod, i + 1)
                for t in range(TB):
                    last = pe.matmul(MB[:, 0:B * E], ONES[:, :], PROD[:, t, :, :].rearrange("p b e -> p (b e)"),
                                     start=(t == 0), stop=(t == TB - 1))
                last.then_inc(sink_sum, 1)
            pe.wait_ge(sink_prod, SINKHORN_ITERS + 1)
            for t in range(TB):
                last = pe.transpose(PVB[0:B * E, P * t:P * t + P], PROD[:, t, :, :].rearrange("p b e -> p (b e)"), IDF[:, :])
            last.then_inc(gt_ready, 1)
            pe.wait_ge(topi_ready, 1)
            pe.transpose(MB[:, 0:B * E], TOPF[:, :, :].rearrange("p a j -> p (a j)"),
                         IDF[0:B * E, 0:B * E]).then_inc(it_ready, 1)
            pe.sem_inc(onehot_used, 2)
            with pe.Fori(0, B) as b:
                for e2 in range(E // 2):
                    pe.wait_ge(onehot, 4 * b + e2 + 1)
                    for t in range(TB):
                        last = pe.matmul(ROWP[0][:, bass.ds(32 * b + (8 * t + 2 * e2), 2)],
                                         OH[e2 % 2][:, P * t:P * t + P], RANKC[:, :], start=True, stop=True)
                    last.then_inc(onehot_used, 1)
            def tiles(b, par):
                pe.wait_ge(xs_ready[par], 8 * (b - par) + 16)
                for t in range(TB):
                    if not isinstance(b, int) or b > 0 or t >= 2:
                        pe.wait_ge(pa_ready, 4 * b + t - 1)
                        pe.wait_ge(lower, 4 * b + t - 1)
                    for half in range(2):
                        last = pe.matmul(CH[t % 2][:, T * half:T * half + T], XS[par][:, P * t:P * t + P],
                                         WEXP[:, 4 * half:4 * half + 4, :].rearrange("p e o -> p (e o)"),
                                         start=True, stop=True)
                    last.then_inc(y_full, 1)
            tiles(0, 0)
            tiles(1, 1)
            with pe.Fori(2, B - 1, 2) as i:
                tiles(i, 0)
                tiles(i + 1, 1)

        @block.scalar
        def _(act):
            def take(bt, name, dst, src):
                act.wait_ge(misc_full, bt.misc(name) + 1)
                act.activation(dst, src, ACT.Copy).then_inc(misc_free, 1)

            def xn_taken(bt): take(bt, "xnT", XNT[:, :], MB[:, :])
            def v_taken(bt):
                dst = VP[1 - bt.par][:, :].rearrange("p (t v) -> p t v", t=TB)[:, :, 0:H * VS]
                for t in range(TB):
                    if t == 0:
                        act.wait_ge(misc_full, bt.misc("v") + 1)
                    last = act.activation(dst[:, t].rearrange("p (h d) -> p h d", d=VS)[:, :, 0:HD],
                                          MB4[:, t].rearrange("p (h d) -> p h d", d=HD), ACT.Copy)
                last.then_inc(misc_free, 1)
            def y_taken(bt): take(bt, "yT", YT[:, :], MB[:, :])
            def xn2_taken(bt):
                if not isinstance(bt.b, int) or bt.b > 1:
                    act.wait_ge(xn2_saved, 16 * bt.b - 16)
                take(bt, "xn2T", XN2S[:, :], MB[:, :])

            def cut(b, w, i):
                act.wait_ge(resid[w], 3 * b + i + 1)
                if i == 0 and not (isinstance(b, int) and b == 0):
                    act.wait_ge(stored[w], 32 * b)
                act.activation(PARTS[w][:, i, :], RES[w][:, :], ACT.Copy).then_inc(part[w], 1)

            def exps(b, s, c):
                act.wait_ge(chunk_ready, 20 * b + 5 * s + c + 1)
                if c == 0 and not (isinstance(b, int) and 4 * b + s < 2):
                    act.wait_ge(pv_done, 4 * b + s - 1)
                act.activation(PT[s % 2][:, c, :], CH[(5 * s + c) % 2][:, :], ACT.Exp).then_inc(exp_done, 1)

            def values_taken(b, s):
                act.wait_ge(pv_done, 4 * b + s + 1)
                act.activation(OT[:, :], PVB[:, :], ACT.Copy).then_inc(pv_copied, 1)

            CUTS = {(0, 4): (0, 0), (1, 0): (0, 1), (1, 1): (0, 2), (1, 2): (1, 0), (1, 3): (1, 1), (1, 4): (1, 2)}
            extras = {"xnT": xn_taken, "v": v_taken, "yT": y_taken, "xn2T": xn2_taken}

            start = Batch(-1, 1, order=MISC_START)
            xn_taken(start)
            for w in range(2):
                for i in range(3):
                    cut(0, w, i)
            act.wait_ge(built, 8)
            v_taken(start)

            def one(bt):
                for s in range(4):
                    vb, vs = (bt.b, s - 1) if s > 0 else (bt.b - 1, 3)
                    for kind, i in STEP:
                        if kind == "c":
                            exps(bt.b, s, i)
                            if bt.nxt and (s, i) in CUTS:
                                cut(bt.b + 1, *CUTS[s, i])
                        elif (kind, i) == ("v", 2) and (s > 0 or bt.prev):
                            values_taken(vb, vs)
                        elif kind == "x" and bt.extra(s, i) in extras:
                            extras[bt.extra(s, i)](bt)

            batches(act, one)
            end = Batch(B, 0, order=MISC_END)
            values_taken(B - 1, 3)
            y_taken(end)
            xn2_taken(end)

            act.wait_ge(w_ready, 1)

            def weigh(b):
                for t in range(TB):
                    act.wait_ge(y_full, 4 * b + t + 1)
                    if not isinstance(b, int) or b > 0 or t >= 2:
                        act.wait_ge(lower, 4 * b + t - 1)
                    for e in range(4):
                        last = act.activation(PA[t % 2][:, e, :], CH[t % 2][:, T + C * e:T + C * e + C], ACT.Copy,
                                              scale=W[:, bass.ds(32 * b + (8 * t + 4 + e), 1)])
                    last.then_inc(pa_ready, 1)
            weigh(0)
            with act.Fori(1, B) as b:
                weigh(b)

        @block.gpsimd
        def _(pool):
            pool.memset(NHALF[:, :], -0.5)
            pool.memset(ONES[:, :], 1.0).then_inc(built, 1)
            pool.memset(ONER[:, :], 1.0).then_inc(built, 1)
            for i in range(2):
                pool.memset(KZ[i][1][:, :, :].rearrange("p a t -> p (a t)").bitcast(U32), 0).then_inc(built, 1)

            def rstd(n, stats, mv, dst, done):
                pool.wait_ge(stats, n)
                pool.nop(nofuse=True)
                pool.tensor_scalar(dst, mv[:, :, 1], LN_EPS, None, ALU.add)
                pool.drain()
                pool.tensor_tensor(dst, dst, NHALF[:, 0:dst.shape[1]], ALU.pow).then_inc(done, 1)

            def rotate(bt, w):
                b = bt.b + 1
                pool.wait_ge(misc_free, bt.misc(("qs", "ks")[w]) + 1)
                if not (isinstance(b, int) and b == 0):
                    pool.wait_ge(part[w], 3 * b)
                pool.tensor_tensor(RES[w][:, :], TC[:, :], TS[:, :], ALU.add).then_inc(resid[w], 1)

            def subtract(b, w, i):
                pool.wait_ge(part[w], 3 * b + i + 1)
                pool.tensor_tensor(RES[w][:, :], RES[w][:, :], PARTS[w][:, i, :], ALU.subtract).then_inc(resid[w], 1)

            def causal(b, s, c):
                pool.wait_ge(exp_done, 20 * b + 5 * s + c + 1)
                pool.nop(nofuse=True)
                p = PT[s % 2][:, c, :]
                if c == 2:
                    views = [(p.rearrange("p (i t) -> p i t", i=4)[:, :, 0:P], 4)]
                else:
                    views = [(p.rearrange("p (i t) -> p i t", i=2)[:, :, 0:P], 2), (p[:, 2 * T - P:2 * T], 1)]
                for v, n in views:
                    pattern = [[0, n], [1, P]] if n > 1 else [[1, P]]
                    last = pool.affine_select(out=v, in_=v, pattern=pattern, compare_op=ALU.is_ge, fill=0.0,
                                              base=0, channel_multiplier=-1)
                last.then_inc(causal_done, 1)

            rstd(1, ln_stats, MV[:, 0:TB], RSTD[:, 0:TB], ln_rstd)
            start = Batch(-1, 1, order=MISC_START)
            for w in range(2):
                rotate(start, w)
                subtract(0, w, 0)
                subtract(0, w, 1)
            rstd(2, ln_stats, MV[:, TB:], RSTD[:, TB:], ln_rstd)

            NEXT_OPS = {(0, 3): lambda bt: rotate(bt, 0),
                        (0, 4): lambda bt: subtract(bt.b + 1, 0, 0),
                        (1, 0): lambda bt: subtract(bt.b + 1, 0, 1),
                        (1, 1): lambda bt: rotate(bt, 1),
                        (1, 2): lambda bt: subtract(bt.b + 1, 1, 0),
                        (1, 3): lambda bt: subtract(bt.b + 1, 1, 1)}

            def one(bt):
                for s in range(4):
                    for c in range(5):
                        causal(bt.b, s, c)
                        if bt.nxt and (s, c) in NEXT_OPS:
                            NEXT_OPS[s, c](bt)
                        if bt.prev and (s, c) == (2, 3):
                            rstd(bt.b, ln2_stats, MV2, RSTD2[:, :], ln2_rstd)

            batches(pool, one)
            rstd(B, ln2_stats, MV2, RSTD2[:, :], ln2_rstd)

            def finish(b, par):
                if not isinstance(b, int) or b >= 2:
                    pool.wait_ge(out_saved[par], 8 * (b - par))
                for t in range(TB):
                    pool.wait_ge(lower, 4 * b + t + 1)
                    pool.tensor_tensor(O1[t % 2][:, :], S2[t % 2][:, 0, :], S2[t % 2][:, 1, :], ALU.add)
                    pool.drain()
                    pool.tensor_tensor(OUTB[par][:, t, :], O1[t % 2][:, :],
                                       X[:, bass.ds(4 * b + t, 1), :].rearrange("p a c -> p (a c)"),
                                       ALU.add).then_inc(tile_out, 1)
            finish(0, 0)
            finish(1, 1)
            with pool.Fori(2, B - 1, 2) as i:
                finish(i, 0)
                finish(i + 1, 1)

        @block.vector
        def _(dve):
            dve.memset(KZ[0][0][:, :, :].rearrange("p a t -> p (a t)").bitcast(U32), 0).then_inc(built, 1)
            dve.memset(KZ[1][0][:, :, :].rearrange("p a t -> p (a t)").bitcast(U32), 0).then_inc(built, 1)

            def tile_of(b, t):
                return X[:, bass.ds(4 * b + t, 1), :].rearrange("p a c -> p (a c)")

            def statistics(tiles, st, mv, done):
                for t, x in enumerate(tiles):
                    dve.bn_stats(out=st[:, t, :], in_=x)
                dve.drain()
                for t in range(len(tiles)):
                    last = dve.bn_aggr(out=mv[:, t, :], in_=st[:, t, :])
                last.then_inc(done, 1)

            def normalize(b, mean, rs, dst, done):
                for t in range(TB):
                    last = dve.tensor_scalar(dst[:, t, :], tile_of(b, t), mean(t), rs(t), ALU.subtract, ALU.mult)
                last.then_inc(done, 1)

            def normalize_x(b):
                normalize(b, lambda t: MV[:, bass.ds(TB * b + t, 1), 0],
                          lambda t: RSTD[:, bass.ds(TB * b + t, 1)], XN, xn_ready)

            def normalize_x2(b):
                dve.wait_ge(ln2_rstd, b + 1)
                normalize(b, lambda t: MV2[:, t, 0:1], lambda t: RSTD2[:, t:t + 1], XN2, xn2_ready)

            def turn(bt, name, i, w, dst):
                b = bt.b + 1
                if i % 2 == 0:
                    if w == 1:
                        dve.wait_ge(resid[0], 3 * b + 1)
                    elif not (isinstance(b, int) and b == 0):
                        dve.wait_ge(resid[1], 3 * b - 2)
                dve.wait_ge(misc_full, bt.misc(name) + 1)
                dve.tensor_tensor(dst[:, :], MB[:, :], ROPE[:, i, :], ALU.mult).then_inc(misc_free, 1)

            def row_maxima(b, s, u):
                dve.wait_ge(rows_ready, 4 * NU * b + NU * s + u + 1)
                dve.nop(nofuse=True)
                for qb, i, col in UNITS[u]:
                    n = P * (qb + 1)
                    last = dve.tensor_tensor_reduce(out=JUNK[u % 2][:, col:col + n], in0=ROWP[u % 2][:, col:col + n],
                                                    in1=TRI[:, T - n:T], scale=1.0, scalar=-3e38,
                                                    op0=ALU.add, op1=ALU.max,
                                                    accum_out=MX[s % 2][:, 4 * qb + i:4 * qb + i + 1])
                last.then_inc(row_max, 1)

            def minus_max(s):
                mx = MX[s % 2][:, :].rearrange("p (a h) -> p a h", h=2)
                dve.drain()
                dve.tensor_scalar(NMX[:, :, :, 0], mx, -1.0, None, ALU.mult)
                dve.drain()
                dve.scalar_tensor_tensor(out=NMX[:, :, :, 1], in0=mx, scalar=-1.0, in1=NMX[:, :, :, 0],
                                         op0=ALU.mult, op1=ALU.subtract).then_inc(nmax_ready, 1)

            def max_rows_taken(bt, par, s):
                dve.wait_ge(misc_full, bt.misc(f"mx{s}") + 1)
                dve.tensor_copy(QP[par][MAX_ROW:MAX_ROW + 4, 2 * s:2 * s + 2, :].rearrange("p a t -> p (a t)"),
                                MBH[MAX_ROW:MAX_ROW + 4, :]).then_inc(misc_free, 1)

            def out_taken(bt, s):
                o = MB[:, :].rearrange("p (t i r) -> p t i r", t=TB, i=4)
                y = Y[:, :, 32 * s:32 * s + 32].rearrange("p t (i d) -> p t i d", i=4)
                dve.wait_ge(misc_full, bt.misc(f"ot{s}") + 1)
                dve.reciprocal(RSUM[:, :, :], o[:, :, :, HD])
                dve.drain()
                dve.tensor_tensor(y, o[:, :, :, 0:HD], RSUM[:, :, :].unsqueeze(3).to_broadcast([P, TB, 4, HD]),
                                  ALU.mult).then_inc(misc_free, 1)

            def add_attention(bt):
                dve.wait_ge(misc_full, bt.misc("proj") + 1)
                xt = X[:, bass.ds(4 * (bt.b - 1), TB), :].rearrange("p t c -> p (t c)")
                dve.tensor_tensor(xt, MB[:, :], xt, ALU.add).then_inc(misc_free, 1)
                dve.drain()
                statistics([tile_of(bt.b - 1, t) for t in range(TB)], ST2, MV2, ln2_stats)

            def clip_logits(bt):
                dve.wait_ge(misc_full, bt.misc("logits") + 1)
                dve.tensor_scalar(LG[:, bass.ds(4 * (bt.b - 1), TB), :].rearrange("p t e -> p (t e)"),
                                  MB[:, 0:TB * E], CLIP_EPS, None, ALU.max).then_inc(misc_free, 1)

            extras = {"q": lambda bt: turn(bt, "q", 0, 0, TC), "qs": lambda bt: turn(bt, "qs", 1, 0, TS),
                      "k": lambda bt: turn(bt, "k", 2, 1, TC), "ks": lambda bt: turn(bt, "ks", 3, 1, TS),
                      "proj": add_attention, "logits": clip_logits}

            dve.wait_ge(x_first, 16)
            statistics([X[:, t, :] for t in range(TB)], ST[:, 0:TB], MV[:, 0:TB], ln_stats)
            dve.wait_ge(ln_rstd, 1)
            normalize_x(0)
            for i in range(2):
                dve.memset(VP[i][:, :], 1.0).then_inc(built, 1)
            dve.wait_ge(ident_loaded, 16)
            dve.wait_ge(weights, 128)
            dve.tensor_copy(IDB[:, :], IDF[:, :])
            dve.tensor_copy(RANKC[:, :], SMALL[:, T:T + 2])
            dve.drain()
            start = Batch(-1, 1, order=MISC_START)
            turn(start, "q", 0, 0, TC)
            turn(start, "qs", 1, 0, TS)
            turn(start, "k", 2, 1, TC)
            turn(start, "ks", 3, 1, TS)
            dve.wait_ge(x_rest, 16 * (B - 1))
            statistics([X[:, t, :] for t in range(TB, B * TB)], ST[:, TB:], MV[:, TB:], ln_stats)
            for u in range(NU):
                row_maxima(0, 0, u)
            minus_max(0)
            max_rows_taken(start, 0, 0)
            dve.wait_ge(ln_rstd, 2)

            def one(bt):
                b, par = bt.b, bt.par
                for s in range(4):
                    nb, npar, ns = (b, par, s + 1) if s < 3 else (b + 1, 1 - par, 0)
                    has_next, has_values = s < 3 or bt.nxt, s > 0 or bt.prev
                    for kind, i in STEP:
                        if kind == "u" and has_next:
                            row_maxima(nb, ns, i)
                        elif kind == "x" and bt.extra(s, i) in extras:
                            extras[bt.extra(s, i)](bt)
                        if (s, kind, i) == (0, "u", 1) and bt.nxt:
                            normalize_x(b + 1)
                        if (s, kind, i) == (2, "u", 9) and bt.prev:
                            normalize_x2(b - 1)
                    if has_next:
                        minus_max(ns)
                    if has_values:
                        out_taken(bt, (s - 1) % 4)
                    if has_next:
                        max_rows_taken(bt, npar, ns)

            batches(dve, one)
            end = Batch(B, 0, order=MISC_END)
            out_taken(end, 3)
            add_attention(end)
            normalize_x2(B - 1)
            clip_logits(end)
            dve.drain()

            def per_token(v):
                return v[:, :].rearrange("p (b t) -> p b t", b=B).unsqueeze(3).to_broadcast([P, B, TB, E])
            prod4 = PROD[:, :, :, :].rearrange("p t b e -> p b t e")
            lg4 = LG[:, :, :].rearrange("p (b t) e -> p b t e", b=B)
            dve.tensor_reduce(out=RSC[:, :], in_=LG[:, :, :], axis=AX.X, op=ALU.max)
            dve.drain()
            dve.reciprocal(RINV[:, :], RSC[:, :])
            dve.drain()
            dve.tensor_tensor(KT[:, :, :, :], lg4, per_token(RINV), ALU.mult)
            dve.drain()
            dve.tensor_tensor(prod4, KT[:, :, :, :], per_token(RSC), ALU.mult).then_inc(sink_prod, 1)

            def rescale(i):
                dve.wait_ge(sink_sum, i + 1)
                dve.reciprocal(CSC[:, :, :].rearrange("p b e -> p (b e)"), MB[:, 0:B * E])
                dve.drain()
                dve.tensor_tensor(SCALED[:, :, :, :], KT[:, :, :, :],
                                  CSC[:, :, :].unsqueeze(2).to_broadcast([P, B, TB, E]), ALU.mult)
                dve.drain()
                dve.tensor_reduce(out=RINV[:, :], in_=SCALED[:, :, :, :].rearrange("p b t e -> p (b t) e"),
                                  axis=AX.X, op=ALU.add)
                dve.drain()
                dve.reciprocal(RSC[:, :], RINV[:, :])
                dve.drain()

            with dve.Fori(0, SINKHORN_ITERS - 1) as i:
                rescale(i)
                dve.tensor_tensor(prod4, KT[:, :, :, :], per_token(RSC), ALU.mult).then_inc(sink_prod, 1)
            rescale(SINKHORN_ITERS - 1)
            dve.tensor_tensor(prod4, SCALED[:, :, :, :], per_token(RSC), ALU.mult).then_inc(sink_prod, 1)

            dve.wait_ge(gt_ready, 1)
            dve.tensor_copy(GT[:, :], PVB[0:B * E, :])
            dve.drain()
            with dve.Fori(0, TOPK - 8, 8) as r:
                dve.max(out=TOPV[:, :], in_=GT[:, :])
                dve.drain()
                dve.max_index(out=TOPI8[:, :], in_max=TOPV[:, :], in_values=GT[:, :])
                dve.match_replace(out=GT[:, :], in_to_replace=TOPV[:, :], in_values=GT[:, :], imm_value=-1.0)
                dve.drain()
                dve.tensor_copy(TOPF[:, 0, bass.ds(r, 8)], TOPI8[:, :])
                dve.tensor_copy(TOPF[:, 1, bass.ds(r, 8)], TOPI8[:, :])
            dve.max(out=TOPV[:, :], in_=GT[:, :])
            dve.drain()
            dve.max_index(out=TOPI8[:, :], in_max=TOPV[:, :], in_values=GT[:, :])
            dve.drain()
            dve.tensor_copy(TOPF[:, 0, TOPK - 8:TOPK], TOPI8[:, :])
            dve.tensor_copy(TOPF[:, 1, TOPK - 8:TOPK], TOPI8[:, :]).then_inc(topi_ready, 1)
            dve.wait_ge(it_ready, 1)
            for half in range(2):
                dve.tensor_copy(IT[64 * half:64 * half + 64, :],
                                MB[64 * half:64 * half + 64, 0:B * E].rearrange("p (c h) -> p c h", h=2)[:, :, half])
            dve.drain()
            with dve.Fori(0, B) as b:
                for e2 in range(E // 2):
                    dve.wait_ge(onehot_used, 4 * b + e2 + 1)
                    dve.tensor_scalar(OH[e2 % 2][:, :], SMALL[:, 0:T], IT[:, bass.ds(4 * b + e2, 1)], None,
                                      ALU.is_equal).then_inc(onehot, 1)

            dve.wait_ge(onehot_used, 2 + 4 * B)
            numbers = SMALL[:, T + 2:T + 2 + E].unsqueeze(1).to_broadcast([P, B * TB, E])
            dve.scalar_tensor_tensor(out=KEY[:, :, :], in0=ROWP[0][:, 0:B * TB * E].rearrange("p (t e) -> p t e", e=E),
                                     scalar=float(E), in1=numbers, op0=ALU.mult, op1=ALU.add)
            dve.drain()
            dve.tensor_reduce(out=KMAX[:, :], in_=KEY[:, :, :], axis=AX.X, op=ALU.max)
            dve.drain()
            dve.tensor_tensor(HARD[:, :, :], KEY[:, :, :], KMAX[:, :].unsqueeze(2).to_broadcast([P, B * TB, E]),
                              ALU.is_equal)
            dve.drain()
            dve.scalar_tensor_tensor(out=HARD[:, :, :], in0=KEY[:, :, :], scalar=float(E), in1=HARD[:, :, :],
                                     op0=ALU.is_ge, op1=ALU.mult)
            dve.drain()
            dve.tensor_scalar(SCALED[:, :, :, :], prod4, 0.5, None, ALU.is_gt)
            dve.drain()
            dve.tensor_tensor(W[:, :], HARD[:, :, :].rearrange("p t e -> p (t e)"),
                              SCALED[:, :, :, :].rearrange("p b t e -> p (b t e)"), ALU.mult).then_inc(w_ready, 1)
            dve.drain()

            def add_lower(b):
                for t in range(TB):
                    dve.wait_ge(y_full, 4 * b + t + 1)
                    dve.wait_ge(pa_ready, 4 * b + t + 1)
                    for e in range(4):
                        dve.scalar_tensor_tensor(out=SS[t % 2][:, e, :], in0=CH[t % 2][:, C * e:C * e + C],
                                                 scalar=W[:, bass.ds(32 * b + (8 * t + e), 1)],
                                                 in1=PA[t % 2][:, e, :], op0=ALU.mult, op1=ALU.add)
                    dve.drain()
                    if not isinstance(b, int) or b > 0 or t >= 2:
                        dve.wait_ge(tile_out, 4 * b + t - 1)
                    dve.tensor_tensor(S2[t % 2][:, :, :], SS[t % 2][:, 0:2, :], SS[t % 2][:, 2:4, :], ALU.add).then_inc(lower, 1)
            add_lower(0)
            with dve.Fori(1, B) as b:
                add_lower(b)


_OUT = (B, T, C)


def _layout():
    half, d, pair = np.meshgrid(np.arange(2), np.arange(HD), np.arange(PAIRS), indexing="ij")
    cols = ((2 * pair + half) * HD + d).reshape(-1)
    swap = ((2 * pair + half) * HD + (d ^ 1)).reshape(-1)
    inv = (np.float32(1.0) / np.float32(10000.0) ** (np.arange(0, HD, 2, dtype=np.float32) / np.float32(HD)))
    freqs = np.arange(T, dtype=np.float32)[:, None] * inv.astype(np.float32)[None, :]
    cos, sin = np.cos(freqs).astype(np.float32), np.sin(freqs).astype(np.float32)
    dd = d.reshape(-1)
    c = cos[:, dd // 2].T
    s = sin[:, dd // 2].T * np.where(dd % 2 == 0, -1.0, 1.0)[:, None].astype(np.float32)
    scale = np.float32(1.0) / np.sqrt(np.float32(HD))
    rope = np.stack([c * scale, s * scale, c, s], axis=1).astype(np.float32)
    tri = np.zeros((P, T), np.float32)
    q, k = np.meshgrid(np.arange(P), np.arange(P), indexing="ij")
    tri[:, T - P:] = np.where(k > q, np.float32(-3e38), np.float32(0))
    small = np.zeros((P, T + 2 + E), np.float32)
    small[:, 0:T] = np.arange(T)
    place = np.arange(P) % TOPK + 1
    small[:, T] = np.where(np.arange(P) < TOPK, place, 0)
    small[:, T + 1] = np.where(np.arange(P) >= TOPK, place, 0)
    small[:, T + 2:] = np.arange(E)
    return cols, swap, rope, tri, small


def kernel(L0_attn_x, L0_attn_W_attn, L0_attn_W_proj, L0_ffn_gate_w, L0_ffn_experts):
    import concourse.bacc as _bacc
    from concourse.bass_utils import run_bass_kernel_spmd as _run

    cols, swap, rope, tri, small = _layout()
    w = np.asarray(L0_attn_W_attn)
    arrays = {
        "x": np.ascontiguousarray(L0_attn_x),
        "w_qkv": np.ascontiguousarray(np.concatenate([w[:, cols], w[:, C + cols], w[:, 2 * C:]], axis=1)),
        "w_swap": np.ascontiguousarray(np.concatenate([w[:, swap], w[:, C + swap]], axis=1)),
        "w_proj": np.ascontiguousarray(L0_attn_W_proj),
        "gate_w": np.ascontiguousarray(np.asarray(L0_ffn_gate_w)[0]),
        "experts": np.ascontiguousarray(L0_ffn_experts),
        "rope": rope, "tri": tri, "ident": np.eye(P, dtype=np.float32), "small": small,
    }
    nc = _bacc.Bacc("TRN2", target_bir_lowering=False, num_devices=1)
    args = [nc.dram_tensor(f"in_{name}", a.shape, mybir.dt.from_np(a.dtype), kind="ExternalInput").ap()
            for name, a in arrays.items()]
    out = nc.dram_tensor("out_0", _OUT, F32, kind="ExternalOutput").ap()
    build(nc, *args, out)
    r = _run(nc, [{f"in_{name}": a for name, a in arrays.items()}], core_ids=[0])
    return r.results[0]["out_0"]
```

```python
import numpy as np
import concourse.bass as bass
from concourse import mybir
from contextlib import ExitStack

F32 = mybir.dt.float32
F16 = mybir.dt.float16
BF16 = mybir.dt.bfloat16
U32 = mybir.dt.uint32
ACT = mybir.ActivationFunctionType
ALU = mybir.AluOpType
AX = mybir.AxisListType

B, T, C = 8, 512, 128
H, HD = 16, 8
E = 8
P = 128
TB = T // P
PAIRS = H // 2
TOPK = T // E
SINKHORN_ITERS = 8
MID = B * E - 2
LN_EPS = 1e-5
CLIP_EPS = 1e-6

Q_PART = [0, 0, 0, 1, 1, 2]
K_PART = [0, 1, 2, 0, 1, 0]
HEAD_ROWS = len(Q_PART) * HD
ROWS_K = 2 * HEAD_ROWS
MAX_ROW = ROWS_K
ALL_K = MAX_ROW + 4
VS = HD + 1
VKB = H * VS + 32

STEP = [("w", 8), ("n", 0), ("n", 1), ("v", 0), ("u", 0), ("w", 9), ("x", 0), ("u", 1), ("u", 2),
        ("v", 3), ("u", 3), ("mx", 0), ("v", 1), ("v", 2), ("u", 4), ("c", 0), ("x", 1), ("u", 5),
        ("c", 1), ("u", 6), ("c", 2), ("x", 2), ("u", 7), ("c", 3), ("c", 4), ("c", 5), ("x", 3),
        ("ot", 0), ("c", 6), ("u", 8), ("c", 7), ("u", 9), ("x", 4)]
LAST_V = [i for kind, i in STEP if kind == "v"][-1]
EXTRAS = {(0, 1): "xnT n", (0, 2): "q n", (0, 3): "qs n", (0, 4): "k n", (1, 0): "ks n",
          (1, 1): "yT p", (1, 2): "proj p", (1, 3): "v n", (2, 4): "xn2T p", (3, 2): "logits p"}
ROTATE = {(0, "c", 4): 0, (1, "u", 2): 1}
CUT = {(1, "x", 0): (0, 0), (1, "v", 1): (1, 0), (1, "c", 1): (1, 1), (1, "u", 6): (0, 1),
       (1, "x", 3): (1, 2)}
CUT_V = {(1, "c", 4): (0, 2)}
SUBTRACT = {(1, "u", 2): (1, 0), (1, "u", 3): (0, 0), (1, "c", 1): (0, 1), (1, "u", 6): (1, 1)}
NORMALIZE = (0, "w", 9)
STATISTICS2 = (2, "w", 9)
RSTD2_AT = (2, "w", 9)
NORMALIZE2 = (2, "u", 6)

UNITS = [[(3, i, 0)] for i in range(4)] + [[(2, i, 0), (0, i, 3 * P)] for i in range(4)] + \
        [[(1, 2 * i, 0), (1, 2 * i + 1, 2 * P)] for i in range(2)]
NU = len(UNITS)
CHUNKS = [[(i, 0, 0)] for i in range(4)] + [[(i, 1, 0), (i, 3, 3 * P)] for i in range(4)] + \
         [[(2 * i, 2, 0), (2 * i + 1, 2, 2 * P)] for i in range(2)]
NC = len(CHUNKS)
AT = {(i, kb): (c, col) for c, parts in enumerate(CHUNKS) for i, kb, col in parts}
BANK = [0, 1, 2, 0, 1, 2, 0, 1, 2, 1]
BACK = [4, 2, 4, 3, 3, 3, 3, 3, 3, 2]
NZ = 8
ZEROED = {0: 2, 1: 6, 3: 6, 2: 8}


def _shared_bank_order():
    order = []
    for s in range(4):
        for kind, i in STEP:
            if kind == "x" and (s, i) in EXTRAS:
                order.append(EXTRAS[s, i])
            elif kind == "mx":
                order.append(f"mx{s}")
            elif kind == "ot":
                order.append(f"ot{s - 1}" if s > 0 else "ot3 p")
    return order


MISC = _shared_bank_order()
MISC_START = ["xnT n"]
MISC_END = ["ot3 p", "yT p", "proj p", "xn2T p", "logits p"]
PREV = sum(m.endswith("p") for m in MISC)
NEXT = sum(m.endswith("n") for m in MISC)


DIRECT = 5
STORED = DIRECT * TB
SHARE = [[3], [3], [3], [2, 3], [2, 3]]
OTHERS = [[t for t in range(TB) if t not in own] for own in SHARE]
DENSE_END, DENSE_SINK = 3, SINKHORN_ITERS


def by_now(b):
    return sum(map(len, SHARE[:b + 1])), sum(map(len, OTHERS[:b + 1]))


class Batch:

    def __init__(self, b, par, prev=True, nxt=True, order=MISC):
        self.b, self.par, self.prev, self.nxt = b, par, prev, nxt
        self.order = [m.split()[0] for m in order
                      if (prev or not m.endswith("p")) and (nxt or not m.endswith("n"))]
        if order is MISC_START:
            self.base = 0
        elif order is MISC_END:
            self.base = b * len(MISC) + len(MISC_START) - PREV - NEXT
        elif not prev:
            self.base = len(MISC_START)
        else:
            self.base = b * len(MISC) + (len(MISC_START) - PREV)

    def extra(self, s, x):
        name, _, kind = EXTRAS.get((s, x), "").partition(" ")
        return name if (kind == "n" and self.nxt) or (kind == "p" and self.prev) else None

    def misc(self, name):
        return self.base + self.order.index(name)


def build(nc, x_in, w_qkv, w_swap, w_proj, gate_w, experts, rope, tri, ident, small, out):
    ctx = ExitStack()
    with ctx:
        def sb(name, shape, dt=F32):
            return ctx.enter_context(nc.sbuf_tensor(name, shape, dt))

        def sem(name):
            return ctx.enter_context(nc.semaphore(name))

        YS = sb("YS", [P, 22 * E * C])
        taken = [0]

        def arena(shape, dt=F32, keep=P):
            n = int(np.prod(shape[1:]))
            words = n if dt == F32 else n // 2
            v = YS[:, taken[0]:taken[0] + words]
            taken[0] += words
            v = v if dt == F32 else v.bitcast(dt)
            if len(shape) == 3:
                v = v.rearrange("p (a t) -> p a t", a=shape[1])
            return v
        KZ = [[arena([P, PAIRS, T], BF16) for h in range(2)] for i in range(2)]
        QP = [arena([P, PAIRS, T], BF16) for i in range(2)]
        PT = [arena([P, NC, T]) for i in range(2)]
        assert STORED * E * C <= taken[0] <= 22 * E * C
        WQKV = sb("WQKV", [P, 3 * C])
        WSWAP = sb("WSWAP", [P, 2 * C])
        WPROJ = sb("WPROJ", [P, C])
        WGATE = sb("WGATE", [P, E])
        WEXP = sb("WEXP", [P, E, C])
        ROPE = sb("ROPE", [P, 4, T])
        TRI = sb("TRI", [P, T])
        IDF = sb("IDF", [P, P])
        IDB = sb("IDB", [P, P], BF16)
        SMALL = sb("SMALL", [P, T + 2 * B * E - 2 + E])
        RANKC = sb("RANKC", [P, 2 * B * E - 2], BF16)
        ONES = sb("ONES", [P, P])
        NHALF = sb("NHALF", [P, B * TB])
        ONER = sb("ONER", [2, PAIRS * T], BF16)
        X = sb("X", [P, B * TB, C])
        LG = sb("LG", [P, B * TB, E])
        VP = [sb(f"VP{i}", [P, TB * VKB]) for i in range(2)]
        XN = sb("XN", [P, TB, C])
        XNT = sb("XNT", [P, T])
        ST = sb("ST", [P, B * TB, 6])
        MV = sb("MV", [P, B * TB, 2])
        RSTD = sb("RSTD", [P, B * TB])
        SHIFT = sb("SHIFT", [P, B * TB])
        TC = sb("TC", [P, T])
        TS = sb("TS", [P, T])
        RES = [sb(f"RES{w}", [P, T]) for w in range(2)]
        PARTS = [sb(f"PARTS{w}", [P, 3, T], BF16) for w in range(2)]
        MX = [sb(f"MX{i}", [P, 16]) for i in range(2)]
        NMX = sb("NMX", [P, 8, 2, 2], BF16)
        JUNK = [sb(f"JUNK{i}", [P, T], BF16) for i in range(3)]
        OT = sb("OT", [P, T])
        RSUM = sb("RSUM", [P, TB, 4])
        Y = sb("Y", [P, TB, C])
        YT = sb("YT", [P, T])
        XN2 = sb("XN2", [P, TB, C])
        ST2 = sb("ST2", [P, TB, 6])
        MV2 = sb("MV2", [P, TB, 2])
        RSTD2 = sb("RSTD2", [P, TB])
        SHIFT2 = sb("SHIFT2", [P, TB])
        XN2S = sb("XN2S", [P, T])
        KT = sb("KT", [P, B, TB, E])
        PROD = sb("PROD", [P, 2, TB, B * E // 2])
        GATES = sb("GATES", [P, TB, B, E])
        SCALED = sb("SCALED", [P, B, TB, E])
        RINV = sb("RINV", [P, B * TB])
        RSC = sb("RSC", [P, B * TB])
        CSUM = sb("CSUM", [P, B, E])
        CSC = sb("CSC", [P, B, E])
        GT = [sb(f"GT{i}", [B * E, T]) for i in range(2)]
        TOPV = [sb(f"TOPV{i}", [B * E, 8]) for i in range(2)]
        TOPI = sb("TOPI", [B * E, TOPK], U32)
        TOPF = sb("TOPF", [B * E, 2, TOPK])
        IT = sb("IT", [P, B * E // 2])
        TOKEN = sb("TOKEN", [P, T], F16)
        OH = [sb(f"OH{i}", [P, T], BF16) for i in range(4)]
        RT = sb("RT", [B * E, T])
        KEY = sb("KEY", [P, TB * B, E])
        KMAX = sb("KMAX", [P, B * TB])
        HARD = sb("HARD", [P, B * TB, E])
        OPEN = sb("OPEN", [P, TB * B, E])
        W = sb("W", [P, TB * B * E])
        XS = [sb(f"XS{i}", [P, T]) for i in range(2)]
        WY = [YS[:, E * C * n:E * C * n + E * C].rearrange("p (e c) -> p e c", e=E)
              for n in (STORED, STORED + 1)]
        SUM4 = sb("SUM4", [P, 4, C])
        SUM2 = sb("SUM2", [P, 2, C])
        SUM1 = sb("SUM1", [P, C])

        CHB = ctx.enter_context(nc.psum_tensor("CHB", [P, 3 * T], F32))
        ROWB = ctx.enter_context(nc.psum_tensor("ROWB", [P, 3 * T], F32))
        CH = [CHB[:, T * i:T * i + T] for i in range(3)]
        ROWP = [ROWB[:, T * i:T * i + T] for i in range(3)]
        PVB = ctx.enter_context(nc.psum_tensor("PVB", [P, T], F32))
        MB = ctx.enter_context(nc.psum_tensor("MB", [P, T], F32))
        MBH = MB[:, :].bitcast(BF16)
        MB4 = MB[:, :].rearrange("p (a c) -> p a c", a=TB)
        SUMS = (MB, PVB)
        FIRSTB = ROWP + CH[0:2]
        EXPB = [CHB[:, 0:2 * T], ROWB[:, 0:2 * T]]
        DIRECTB = [(CH[0], CH[1]), (ROWP[0], ROWP[1]), (CH[2], PVB[:, :]), (ROWP[2], MB[:, :])]

        xn2_dram = nc.dram_tensor("xn2_scratch", [B, P, T], F32, kind="Internal").ap()
        scratch = nc.dram_tensor("parts_scratch", [2, 2, 2, 3, HD, PAIRS, T], BF16, kind="Internal").ap()

        ident_loaded = sem("ident_loaded")
        x_first = sem("x_first_loaded")
        x_rest = sem("x_rest_loaded")
        weights = sem("weights_loaded")
        tables = sem("tables_loaded")
        later_weights = sem("later_weights_loaded")
        first_full = sem("first_projections")
        built = sem("constants_built")
        first_turned = sem("first_turned")
        one_rows = sem("one_rows_loaded")
        rows_ready = sem("score_rows_ready")
        row_max = sem("row_max_done")
        nmax_high = sem("minus_max_high")
        nmax_ready = sem("minus_max_ready")
        chunk_ready = sem("score_chunk_ready")
        exp_done = sem("exp_done")
        causal_done = sem("causal_done")
        pv_done = sem("pv_done")
        pv_copied = sem("pv_copied")
        misc_full = sem("misc_full")
        misc_free = sem("misc_free")
        ln_stats = sem("ln_stats")
        ln_rstd = sem("ln_rstd")
        xn_ready = sem("xn_ready")
        ln2_stats = sem("ln2_stats")
        ln2_rstd = sem("ln2_rstd")
        xn2_ready = sem("xn2_ready")
        resid = [sem("q_residual"), sem("k_residual")]
        part = [sem("q_part"), sem("k_part")]
        xn2_saved = sem("xn2_saved")
        stored = [sem("q_stored"), sem("k_stored")]
        loaded = [sem("q_loaded"), sem("k_loaded")]
        sink_prod = [sem(f"sinkhorn_product_{h}") for h in range(2)]
        sink_sum = [sem(f"sinkhorn_sum_{h}") for h in range(2)]
        sink_step = [sem(f"sinkhorn_step_{h}") for h in range(2)]
        gt_ready = sem("gates_transposed")
        top_found = sem("top_eight_found")
        top_placed = sem("top_eight_placed")
        top_removed = sem("top_eight_removed")
        topi_ready = sem("top_indices")
        it_ready = sem("indices_transposed")
        onehot = sem("onehot_ready")
        onehot_used = sem("onehot_used")
        w_ready = sem("weights_of_experts")
        xs_ready = [sem("xn2_even_loaded"), sem("xn2_odd_loaded")]
        y_full = sem("expert_outputs")
        y_copied = sem("expert_outputs_copied")
        rt_ready = sem("ranks_in_sbuf")
        ranks_turned = sem("ranks_turned")
        chain = sem("weighted_sum_step")
        weighted = sem("tile_weighted")
        folded = sem("tile_folded")
        out_saved = sem("out_saved")

        block = ctx.enter_context(nc.Block())

        def weight(b, t, e):
            i = B * E * t + E * b + e
            return W[:, i:i + 1]

        def outputs(n, e):
            return YS[:, C * (E * n + e):C * (E * n + e) + C]

        def batches(eng, one):
            one(Batch(0, 0, prev=False))
            with eng.Fori(1, B - 2, 2) as i:
                one(Batch(i, 1))
                one(Batch(i + 1, 0))
            one(Batch(B - 1, 1, nxt=False))

        def trip(queue, b, par, w, used):
            queue.wait_ge(part[w], 3 * b + 3)
            if used:
                queue.wait_ge(chunk_ready, 4 * NC * b - 4 * NC)
            sc = scratch[w, par]
            for h in range(2):
                queue.dma_start(sc[h].rearrange("n d a t -> (d a) n t"),
                             PARTS[w][64 * h:64 * h + 64, :, :]).then_inc(stored[w], 16)
            queue.wait_ge(stored[w], 32 * b + 32)
            for h in range(2):
                rows = (QP[par] if w == 0 else KZ[par][h])[:, :, :].rearrange("p a t -> p (a t)")
                for i, n in ((0, 3), (1, 2), (2, 1)):
                    slot = Q_PART.index(i)
                    r = HEAD_ROWS * h + HD * slot
                    if w == 0:
                        src = sc[h, i].rearrange("d a t -> d (a t)")
                        src = bass.AP(tensor=src.tensor, offset=src.offset,
                                      ap=[[0, n]] + [list(x) for x in src.ap])
                    else:
                        src = sc[h, 0:n].rearrange("n d a t -> (n d) (a t)")
                    queue.dma_start(rows[r:r + HD * n, :], src).then_inc(loaded[w], 16)

        @block.sync
        def _(sp):
            xv = x_in.rearrange("b (t p) c -> b p t c", p=P)
            Xv = [X[:, TB * b:TB * b + TB, :] for b in range(B)]
            sp.dma_start(Xv[0], xv[0]).then_inc(x_first, 16)
            sp.dma_start(IDF[:, :], ident).then_inc(ident_loaded, 16)
            sp.dma_start(WQKV[:, :], w_qkv).then_inc(weights, 16)
            sp.dma_start(WSWAP[:, :], w_swap).then_inc(weights, 16)
            sp.dma_start(ROPE[:, :, :], rope).then_inc(weights, 16)
            sp.dma_start(TRI[:, :], tri).then_inc(tables, 16)
            sp.dma_start(SMALL[:, :], small).then_inc(tables, 16)
            sp.dma_start(WPROJ[:, :], w_proj).then_inc(later_weights, 16)
            sp.dma_start(WGATE[:, :], gate_w).then_inc(later_weights, 16)
            for b in range(1, B):
                sp.dma_start(Xv[b], xv[b]).then_inc(x_rest, 16)
            sp.dma_start(WEXP[:, :, :], experts.rearrange("e d o -> d e o")).then_inc(later_weights, 16)
            sp.wait_ge(built, 8)
            for i in range(2):
                for h in range(2):
                    r = MAX_ROW + 2 * h
                    sp.dma_start(KZ[i][h][r:r + 2, :, :].rearrange("p a t -> p (a t)"),
                                 ONER[:, :]).then_inc(one_rows, 16)

            trip(sp, 0, 0, 0, False)

            def one(bt):
                if bt.nxt:
                    trip(sp, bt.b + 1, 1 - bt.par, 0, bt.prev)
                    trip(sp, bt.b + 1, 1 - bt.par, 1, bt.prev)
                if bt.prev:
                    save_xn2(bt)

            def save_xn2(bt):
                sp.wait_ge(misc_free, bt.misc("xn2T") + 1)
                sp.dma_start(xn2_dram[bass.ds(bt.b - 1, 1), :, :].rearrange("a p t -> p (a t)"),
                             XN2S[:, :]).then_inc(xn2_saved, 16)

            batches(sp, one)

            def load_xn2(b):
                sp.dma_start(XS[b % 2][:, :], xn2_dram[b]).then_inc(xs_ready[b % 2], 16)

            sp.wait_ge(xn2_saved, 16 * (B - 1))
            load_xn2(0)
            load_xn2(1)
            save_xn2(Batch(B, 0, order=MISC_END))
            for b in range(2, B):
                sp.wait_ge(y_full, TB * (b - 1))
                if b == B - 1:
                    sp.wait_ge(xn2_saved, 16 * B)
                load_xn2(b)
            for b in list(range(DIRECT, B)) + list(range(DIRECT)):
                if b >= DIRECT:
                    sp.wait_ge(chain, TB * E * (b - DIRECT + 1))
                else:
                    own, others = by_now(b)
                    own = min(own + own % 2, by_now(DIRECT - 1)[0])
                    sp.wait_ge(chain, TB * E * (B - DIRECT) + E * own)
                    sp.wait_ge(folded, 4 * others)
                sp.dma_start(out[b].rearrange("(t p) c -> p t c", p=P), X[:, TB * b:TB * b + TB, :]).then_inc(out_saved, 16)
            sp.wait_ge(out_saved, 16 * B)

        @block.tensor
        def _(pe):
            def misc(bt, name):
                n = bt.misc(name)
                if not isinstance(n, int) or n > 0:
                    pe.wait_ge(misc_free, n)

            def score_rows(b, par, s, u):
                n = 4 * NU * b + NU * s + u
                if s == 0 and u == 0:
                    pe.wait_ge(loaded[0], 96 * b + 96)
                    pe.wait_ge(loaded[1], 96 * b + 96)
                if not isinstance(b, int) or n >= BACK[u]:
                    pe.wait_ge(row_max, n + 1 - BACK[u])
                for qb, i, col in UNITS[u]:
                    pair, keys = 2 * s + i // 2, P * (qb + 1)
                    last = pe.matmul(ROWP[BANK[u]][:, col:col + keys], QP[par][0:ROWS_K, pair, P * qb:keys],
                                     KZ[par][i % 2][0:ROWS_K, pair, 0:keys], start=True, stop=True)
                last.then_inc(rows_ready, 1)

            def chunk(b, par, s, c, bt):
                n = 4 * NC * b + NC * s + c
                if c == 0:
                    pe.wait_ge(misc_free, bt.misc(f"mx{s}") + 1)
                if not isinstance(b, int) or n >= BACK[c]:
                    pe.wait_ge(exp_done, n + 1 - BACK[c])
                for i, kb, col in CHUNKS[c]:
                    pair, n = 2 * s + i // 2, T - P * kb
                    last = pe.matmul(CH[BANK[c]][:, col:col + n], KZ[par][i % 2][0:ALL_K, pair, P * kb:P * kb + P],
                                     QP[par][0:ALL_K, pair, P * kb:T], start=True, stop=True)
                last.then_inc(chunk_ready, 1)

            def values(b, par, s, kb):
                pe.wait_ge(causal_done, NZ * (4 * b + s) + ZEROED[kb])
                if kb == 0 and not (isinstance(b, int) and 4 * b + s == 0):
                    pe.wait_ge(pv_copied, 4 * b + s)
                for i in range(4):
                    c, col = AT[i, kb]
                    v = VKB * kb + VS * (4 * s + i)
                    last = pe.matmul(PVB[32 * i:32 * i + 32, P * kb:T], VP[par][:, v:v + 32],
                                     PT[s % 2][:, c, col:col + T - P * kb],
                                     start=(kb == 0), stop=(kb == LAST_V))
                if kb == LAST_V:
                    last.then_inc(pv_done, 1)

            def transposes(src):
                for t in range(TB):
                    last = pe.transpose(MB[:, P * t:P * t + P], src(t), IDF[:, :])
                return last

            def out_transposed(bt, b, s, name):
                misc(bt, name)
                pe.wait_ge(pv_copied, 4 * b + s + 1)
                transposes(lambda t: OT[:, P * t:P * t + P]).then_inc(misc_full, 1)

            def max_rows(bt, b, s):
                misc(bt, f"mx{s}")
                pe.wait_ge(nmax_ready, 4 * b + s + 1)
                for j in range(2):
                    for qb in range(TB):
                        col = T * j + P * qb
                        last = pe.transpose(MBH[MAX_ROW:MAX_ROW + 4, col:col + P],
                                            NMX[:, 2 * qb + j, :, :].rearrange("p h n -> p (h n)"), IDB[:, :])
                last.then_inc(misc_full, 1)

            def xn_transposed(bt):
                misc(bt, "xnT")
                pe.wait_ge(xn_ready, bt.b + 2)
                transposes(lambda t: XN[:, t, :]).then_inc(misc_full, 1)

            def project(bt, name, weight):
                misc(bt, name)
                pe.matmul(MB[:, :], weight, XNT[:, :], start=True, stop=True).then_inc(misc_full, 1)

            def q(bt): project(bt, "q", WQKV[:, 0:C])
            def qs(bt): project(bt, "qs", WSWAP[:, 0:C])
            def k(bt): project(bt, "k", WQKV[:, C:2 * C])
            def ks(bt): project(bt, "ks", WSWAP[:, C:2 * C])

            def by_tiles(bt, name, src, weight, n):
                misc(bt, name)
                for t in range(TB):
                    last = pe.matmul(MB[:, n * t:n * t + n], src[:, P * t:P * t + P], weight,
                                     start=True, stop=True)
                last.then_inc(misc_full, 1)

            def v(bt): by_tiles(bt, "v", XNT, WQKV[:, 2 * C:3 * C], C)
            def y_transposed(bt):
                misc(bt, "yT")
                transposes(lambda t: Y[:, t, :]).then_inc(misc_full, 1)
            def proj(bt): by_tiles(bt, "proj", YT, WPROJ[:, :], C)
            def xn2_transposed(bt):
                misc(bt, "xn2T")
                pe.wait_ge(xn2_ready, bt.b)
                transposes(lambda t: XN2[:, t, :]).then_inc(misc_full, 1)
            def logits(bt): by_tiles(bt, "logits", XN2S, WGATE[:, :], E)

            extras = {"xnT": xn_transposed, "q": q, "qs": qs, "k": k, "ks": ks, "v": v,
                      "yT": y_transposed, "proj": proj, "xn2T": xn2_transposed, "logits": logits}

            pe.wait_ge(ident_loaded, 16)
            start = Batch(-1, 1, order=MISC_START)
            xn_transposed(start)
            pe.wait_ge(weights, 48)
            pe.wait_ge(misc_free, 1)
            for w, bank in zip((WQKV[:, 0:C], WSWAP[:, 0:C], WQKV[:, C:2 * C], WSWAP[:, C:2 * C]), FIRSTB):
                pe.matmul(bank, w, XNT[:, :], start=True, stop=True).then_inc(first_full, 1)
            for t in range(TB):
                last = pe.matmul(FIRSTB[4][:, C * t:C * t + C], XNT[:, P * t:P * t + P], WQKV[:, 2 * C:3 * C],
                                 start=True, stop=True)
            last.then_inc(first_full, 1)
            pe.wait_ge(later_weights, 48)
            pe.wait_ge(built, 8)
            for u in range(NU):
                score_rows(0, 0, 0, u)
            pe.wait_ge(one_rows, 64)

            def one(bt):
                b, par = bt.b, bt.par
                for s in range(4):
                    nb, npar, ns = (b, par, s + 1) if s < 3 else (b + 1, 1 - par, 0)
                    vb, vpar, vs = (b, par, s - 1) if s > 0 else (b - 1, 1 - par, 3)
                    has_next, has_values = s < 3 or bt.nxt, s > 0 or bt.prev
                    for kind, i in STEP:
                        if kind == "u" and has_next:
                            score_rows(nb, npar, ns, i)
                        elif kind == "mx":
                            max_rows(bt, b, s)
                        elif kind == "c":
                            chunk(b, par, s, i, bt)
                        elif kind == "w" and has_values:
                            chunk(vb, vpar, vs, i, bt)
                        elif kind == "v" and has_values:
                            values(vb, vpar, vs, i)
                        elif kind == "ot" and has_values:
                            out_transposed(bt, vb, vs, f"ot{vs}")
                        elif kind == "x" and bt.extra(s, i):
                            extras[bt.extra(s, i)](bt)

            batches(pe, one)
            end = Batch(B, 0, order=MISC_END)

            def buffer(n, half):
                if n < STORED:
                    return EXPB[n % 2][:, T * half:T * half + T]
                return DIRECTB[n % 4][half]

            def experts_of(n, half):
                b, t = n // TB, n % TB
                if half == 0:
                    pe.wait_ge(xs_ready[b % 2], 16 * (b // 2 + 1))
                    if 2 <= n < STORED + 2:
                        pe.wait_ge(y_copied, n - 1)
                    elif n == STORED + 3:
                        pe.wait_ge(w_ready, 1)
                    elif n >= STORED + 4:
                        pe.wait_ge(chain, E * 2 * ((n - STORED - 4) // 2 + 1))
                last = pe.matmul(buffer(n, half), XS[b % 2][:, P * t:P * t + P],
                                 WEXP[:, 4 * half:4 * half + 4, :].rearrange("p e o -> p (e o)"),
                                 start=True, stop=True)
                if half == 1:
                    last.then_inc(y_full, 1)

            step = [0]

            def experts_next(halves):
                for _ in range(halves):
                    experts_of(step[0] // 2, step[0] % 2)
                    step[0] += 1

            for kind, i in STEP:
                if kind == "w":
                    chunk(B - 1, 1, 3, i, end)
                elif kind == "v":
                    values(B - 1, 1, 3, i)
            experts_next(1)
            out_transposed(end, B - 1, 3, "ot3")
            y_transposed(end)
            experts_next(1)
            proj(end)
            experts_next(2 * DENSE_END - 2)
            xn2_transposed(end)
            logits(end)

            for i in range(SINKHORN_ITERS):
                for h in range(2):
                    pe.wait_ge(sink_prod[h], i + 1)
                    pe.matmul(SUMS[h][:, 0:TB * B * E // 2], ONES[:, :], PROD[:, h, :, :].rearrange("p t c -> p (t c)"),
                              start=True, stop=True).then_inc(sink_sum[h], 1)
                    experts_next(1)
            for h in range(2):
                pe.wait_ge(sink_prod[h], SINKHORN_ITERS + 1)
            for t in range(TB):
                last = pe.transpose(CH[2][0:B * E, P * t:P * t + P],
                                    GATES[:, t, :, :].rearrange("p b e -> p (b e)"), IDF[:, :])
            last.then_inc(gt_ready, 1)
            experts_next(2 * (STORED - DENSE_END - DENSE_SINK))
            pe.wait_ge(topi_ready, 1)
            pe.transpose(MB[:, 0:B * E], TOPF[:, :, :].rearrange("p a j -> p (a j)"),
                         IDF[0:B * E, 0:B * E]).then_inc(it_ready, 1)
            pe.sem_inc(onehot_used, 4)
            for j in range(B * E // 2):
                pe.wait_ge(onehot, j + 1)
                last = pe.matmul(ROWP[2][0:B * E, :], RANKC[:, MID - 2 * j:MID - 2 * j + B * E], OH[j % 4][:, :],
                                 start=(j == 0), stop=(j == B * E // 2 - 1)).then_inc(onehot_used, 1)
            pe.wait_ge(rt_ready, 1)
            for t in range(TB):
                last = pe.transpose(MB[:, B * E * t:B * E * t + B * E], RT[:, P * t:P * t + P], IDF[0:B * E, 0:B * E])
            last.then_inc(ranks_turned, 1)
            experts_next(2 * (B * TB - STORED))

        @block.scalar
        def _(act):
            def take(bt, name, dst, src):
                act.wait_ge(misc_full, bt.misc(name) + 1)
                act.activation(dst, src, ACT.Copy).then_inc(misc_free, 1)

            def xn_taken(bt): take(bt, "xnT", XNT[:, :], MB[:, :])
            def v_taken(bt):
                dst = VP[1 - bt.par][:, :].rearrange("p (t v) -> p t v", t=TB)[:, :, 0:H * VS]
                act.wait_ge(misc_full, bt.misc("v") + 1)
                spread_v(dst, MB4).then_inc(misc_free, 1)

            def spread_v(dst, src):
                for t in range(TB):
                    last = act.activation(dst[:, t].rearrange("p (h d) -> p h d", d=VS)[:, :, 0:HD],
                                          src[:, t].rearrange("p (h d) -> p h d", d=HD), ACT.Copy)
                return last
            def normalize_x(b):
                for t in range(TB):
                    tile = bass.ds(TB * b + t, 1)
                    last = act.activation(XN[:, t, :], X[:, tile, :].rearrange("p a c -> p (a c)"), ACT.Identity,
                                          scale=RSTD[:, tile], bias=SHIFT[:, tile])
                last.then_inc(xn_ready, 1)

            def normalize_x2(b):
                act.wait_ge(ln2_rstd, b + 1)
                for t in range(TB):
                    last = act.activation(XN2[:, t, :], X[:, bass.ds(TB * b + t, 1), :].rearrange("p a c -> p (a c)"),
                                          ACT.Identity, scale=RSTD2[:, t:t + 1], bias=SHIFT2[:, t:t + 1])
                last.then_inc(xn2_ready, 1)

            def y_taken(bt): take(bt, "yT", YT[:, :], MB[:, :])
            def xn2_taken(bt):
                if not isinstance(bt.b, int) or bt.b > 1:
                    act.wait_ge(xn2_saved, 16 * bt.b - 16)
                take(bt, "xn2T", XN2S[:, :], MB[:, :])

            def cut(b, w, i):
                act.wait_ge(resid[w], 3 * b + i + 1)
                if i == 0 and not (isinstance(b, int) and b == 0):
                    act.wait_ge(stored[w], 32 * b)
                act.activation(PARTS[w][:, i, :], RES[w][:, :], ACT.Copy).then_inc(part[w], 1)

            def exps(b, s, c):
                act.wait_ge(chunk_ready, 4 * NC * b + NC * s + c + 1)
                if c == 0 and not (isinstance(b, int) and 4 * b + s < 2):
                    act.wait_ge(pv_done, 4 * b + s - 1)
                act.activation(PT[s % 2][:, c, :], CH[BANK[c]], ACT.Exp).then_inc(exp_done, 1)

            def max_rows_taken(bt, par, s):
                take(bt, f"mx{s}", QP[par][MAX_ROW:MAX_ROW + 4, 2 * s:2 * s + 2, :].rearrange("p a t -> p (a t)"),
                     MBH[MAX_ROW:MAX_ROW + 4, :])

            def values_taken(b, s):
                act.wait_ge(pv_done, 4 * b + s + 1)
                act.activation(OT[:, :], PVB[:, :], ACT.Copy).then_inc(pv_copied, 1)

            extras = {"xnT": xn_taken, "v": v_taken, "yT": y_taken, "xn2T": xn2_taken}

            start = Batch(-1, 1, order=MISC_START)
            xn_taken(start)
            act.wait_ge(built, 8)
            act.wait_ge(first_full, 5)
            spread_v(VP[0][:, :].rearrange("p (t v) -> p t v", t=TB)[:, :, 0:H * VS],
                     FIRSTB[4].rearrange("p (a c) -> p a c", a=TB))
            trip(act, 0, 0, 1, False)

            def one(bt):
                for s in range(4):
                    vb, vs = (bt.b, s - 1) if s > 0 else (bt.b - 1, 3)
                    for kind, i in STEP:
                        if kind == "c":
                            exps(bt.b, s, i)
                        elif kind == "w" and (s > 0 or bt.prev):
                            exps(vb, vs, i)
                        elif kind == "mx":
                            max_rows_taken(bt, bt.par, s)
                        elif (kind, i) == ("v", LAST_V) and (s > 0 or bt.prev):
                            values_taken(vb, vs)
                        elif kind == "x" and bt.extra(s, i) in extras:
                            extras[bt.extra(s, i)](bt)
                        if bt.nxt and (s, kind, i) in CUT:
                            cut(bt.b + 1, *CUT[s, kind, i])
                        if bt.nxt and (s, kind, i) == NORMALIZE:
                            normalize_x(bt.b + 1)
                        if bt.prev and (s, kind, i) == NORMALIZE2:
                            normalize_x2(bt.b - 1)

            act.wait_ge(ln_rstd, 2)
            batches(act, one)
            end = Batch(B, 0, order=MISC_END)

            def copy_outputs(n):
                act.wait_ge(y_full, n + 1)
                act.activation(YS[:, E * C * n:E * C * n + E * C], EXPB[n % 2], ACT.Copy).then_inc(y_copied, 1)

            exps(B - 1, 3, 8)
            exps(B - 1, 3, 9)
            values_taken(B - 1, 3)
            y_taken(end)
            copy_outputs(0)
            normalize_x2(B - 1)
            copy_outputs(1)
            xn2_taken(end)
            for n in range(2, STORED):
                copy_outputs(n)
            act.wait_ge(w_ready, 1)
            order = [(b, t) for b in range(DIRECT) for t in OTHERS[b]]
            for j, (b, t) in enumerate(order):
                if j >= 2:
                    act.wait_ge(folded, 4 * (j - 2) + 1)
                for e in range(E):
                    last = act.activation(WY[j % 2][:, e, :], outputs(TB * b + t, e), ACT.Copy, scale=weight(b, t, e))
                last.then_inc(weighted, 1)

        @block.gpsimd
        def _(pool):
            pool.memset(NHALF[:, :], -0.5)
            pool.memset(ONES[:, :], 1.0).then_inc(built, 1)

            def rstd(n, stats, mv, dst, shift, done):
                pool.wait_ge(stats, n)
                pool.nop(nofuse=True)
                pool.tensor_scalar(dst, mv[:, :, 1], LN_EPS, None, ALU.add)
                pool.tensor_scalar(shift, mv[:, :, 0], -1.0, None, ALU.mult)
                pool.drain()
                pool.tensor_tensor(dst, dst, NHALF[:, 0:dst.shape[1]], ALU.pow)
                pool.drain()
                pool.tensor_tensor(shift, shift, dst, ALU.mult).then_inc(done, 1)

            def rotate(bt, w):
                b = bt.b + 1
                pool.wait_ge(misc_free, bt.misc(("qs", "ks")[w]) + 1)
                if not (isinstance(b, int) and b == 0):
                    pool.wait_ge(part[w], 3 * b)
                pool.tensor_tensor(RES[w][:, :], TC[:, :], TS[:, :], ALU.add).then_inc(resid[w], 1)

            def subtract(b, w, i):
                pool.wait_ge(part[w], 3 * b + i + 1)
                pool.tensor_tensor(RES[w][:, :], RES[w][:, :], PARTS[w][:, i, :], ALU.subtract).then_inc(resid[w], 1)

            def causal(b, s, z):
                c = z + 2 if z >= 2 else 2 * z + 1
                pool.wait_ge(exp_done, 4 * NC * b + NC * s + c + 1)
                pool.nop(nofuse=True)
                if z < 2:
                    v = PT[s % 2][:, c - 1:c + 1, 0:P]
                else:
                    cols = [col // P for _, _, col in CHUNKS[c]]
                    v = PT[s % 2][:, c, :].rearrange("p (a t) -> p a t", a=TB)[:, 0:TB:cols[1] - cols[0], :]
                pool.affine_select(out=v, in_=v, pattern=[[0, 2], [1, P]], compare_op=ALU.is_ge, fill=0.0,
                                   base=0, channel_multiplier=-1).then_inc(causal_done, 1)

            rstd(1, ln_stats, MV[:, 0:TB], RSTD[:, 0:TB], SHIFT[:, 0:TB], ln_rstd)
            pool.memset(ONER[:, :], 1.0).then_inc(built, 1)
            for i in range(2):
                pool.memset(KZ[i][1][:, :, :].rearrange("p a t -> p (a t)").bitcast(U32), 0).then_inc(built, 1)
            rstd(2, ln_stats, MV[:, TB:], RSTD[:, TB:], SHIFT[:, TB:], ln_rstd)

            def one(bt):
                for s in range(4):
                    for kind, i in STEP:
                        vb, vs = (bt.b, s - 1) if s > 0 else (bt.b - 1, 3)
                        if kind == "c" and (i >= 4 or i % 2 == 1):
                            causal(bt.b, s, i - 2 if i >= 4 else i // 2)
                        if kind == "w" and (s > 0 or bt.prev):
                            causal(vb, vs, i - 2)
                        if bt.nxt and (s, kind, i) in ROTATE:
                            rotate(bt, ROTATE[s, kind, i])
                        if bt.nxt and (s, kind, i) in SUBTRACT:
                            subtract(bt.b + 1, *SUBTRACT[s, kind, i])
                        if bt.prev and (s, kind, i) == RSTD2_AT:
                            rstd(bt.b, ln2_stats, MV2, RSTD2[:, :], SHIFT2[:, :], ln2_rstd)

            batches(pool, one)
            causal(B - 1, 3, 6)
            causal(B - 1, 3, 7)
            rstd(B, ln2_stats, MV2, RSTD2[:, :], SHIFT2[:, :], ln2_rstd)

            order = [(b, t) for b in range(DIRECT) for t in OTHERS[b]]
            for j, (b, t) in enumerate(order):
                x = X[:, TB * b + t, :]
                pool.wait_ge(weighted, j + 1)
                pool.tensor_tensor(SUM4[:, :, :], WY[j % 2][:, 0:4, :], WY[j % 2][:, 4:8, :], ALU.add).then_inc(folded, 1)
                pool.wait_ge(folded, 4 * j + 1)
                pool.tensor_tensor(SUM2[:, :, :], SUM4[:, 0:2, :], SUM4[:, 2:4, :], ALU.add).then_inc(folded, 1)
                pool.wait_ge(folded, 4 * j + 2)
                pool.tensor_tensor(SUM1[:, :], SUM2[:, 0, :], SUM2[:, 1, :], ALU.add).then_inc(folded, 1)
                pool.wait_ge(folded, 4 * j + 3)
                pool.tensor_tensor(x, SUM1[:, :], x, ALU.add).then_inc(folded, 1)

        @block.vector
        def _(dve):
            dve.memset(KZ[0][0][:, :, :].rearrange("p a t -> p (a t)").bitcast(U32), 0).then_inc(built, 1)
            dve.memset(KZ[1][0][:, :, :].rearrange("p a t -> p (a t)").bitcast(U32), 0).then_inc(built, 1)

            def tile_of(b, t):
                return X[:, bass.ds(4 * b + t, 1), :].rearrange("p a c -> p (a c)")

            def statistics(tiles, st, mv, done):
                for t, x in enumerate(tiles):
                    dve.bn_stats(out=st[:, t, :], in_=x)
                dve.drain()
                for t in range(len(tiles)):
                    last = dve.bn_aggr(out=mv[:, t, :], in_=st[:, t, :])
                last.then_inc(done, 1)

            def cut(b, w, i):
                dve.wait_ge(resid[w], 3 * b + i + 1)
                if i == 0:
                    dve.wait_ge(stored[w], 32 * b)
                dve.tensor_copy(PARTS[w][:, i, :], RES[w][:, :]).then_inc(part[w], 1)

            def turn(bt, name, i, w, dst):
                b = bt.b + 1
                if i % 2 == 0:
                    if w == 1:
                        dve.wait_ge(resid[0], 3 * b + 1)
                    elif not (isinstance(b, int) and b == 0):
                        dve.wait_ge(resid[1], 3 * b - 2)
                dve.wait_ge(misc_full, bt.misc(name) + 1)
                dve.tensor_tensor(dst[:, :], MB[:, :], ROPE[:, i, :], ALU.mult).then_inc(misc_free, 1)

            def row_maxima(b, s, u):
                dve.wait_ge(rows_ready, 4 * NU * b + NU * s + u + 1)
                dve.nop(nofuse=True)
                for qb, i, col in UNITS[u]:
                    n = P * (qb + 1)
                    last = dve.tensor_tensor_reduce(out=JUNK[BANK[u]][:, col:col + n], in0=ROWP[BANK[u]][:, col:col + n],
                                                    in1=TRI[:, T - n:T], scale=1.0, scalar=-3e38,
                                                    op0=ALU.add, op1=ALU.max,
                                                    accum_out=MX[s % 2][:, 4 * qb + i:4 * qb + i + 1])
                last.then_inc(row_max, 1)

            def minus_max(b, s, half):
                mx = MX[s % 2][:, :].rearrange("p (a h) -> p a h", h=2)
                if half == 0:
                    dve.wait_ge(row_max, NU * (4 * b + s + 1))
                    dve.tensor_scalar(NMX[:, :, :, 0], mx, -1.0, None, ALU.mult).then_inc(nmax_high, 1)
                else:
                    dve.wait_ge(nmax_high, 4 * b + s + 1)
                    dve.scalar_tensor_tensor(out=NMX[:, :, :, 1], in0=mx, scalar=-1.0, in1=NMX[:, :, :, 0],
                                             op0=ALU.mult, op1=ALU.subtract).then_inc(nmax_ready, 1)

            def out_taken(bt, s):
                o = MB[:, :].rearrange("p (t i r) -> p t i r", t=TB, i=4)
                y = Y[:, :, 32 * s:32 * s + 32].rearrange("p t (i d) -> p t i d", i=4)
                dve.wait_ge(misc_full, bt.misc(f"ot{s}") + 1)
                dve.reciprocal(RSUM[:, :, :], o[:, :, :, HD])
                dve.drain()
                dve.tensor_tensor(y, o[:, :, :, 0:HD], RSUM[:, :, :].unsqueeze(3).to_broadcast([P, TB, 4, HD]),
                                  ALU.mult).then_inc(misc_free, 1)

            def add_attention(bt):
                dve.wait_ge(misc_full, bt.misc("proj") + 1)
                xt = X[:, bass.ds(4 * (bt.b - 1), TB), :].rearrange("p t c -> p (t c)")
                dve.tensor_tensor(xt, MB[:, :], xt, ALU.add).then_inc(misc_free, 1)

            def statistics2(bt):
                b = bt.b - 1
                dve.wait_ge(misc_free, bt.misc("proj") + 1)
                dve.nop(nofuse=True)
                statistics([tile_of(b, t) for t in range(TB)], ST2, MV2, ln2_stats)

            def clip_logits(bt):
                dve.wait_ge(misc_full, bt.misc("logits") + 1)
                dve.tensor_scalar(LG[:, bass.ds(4 * (bt.b - 1), TB), :].rearrange("p t e -> p (t e)"),
                                  MB[:, 0:TB * E], CLIP_EPS, None, ALU.max).then_inc(misc_free, 1)

            extras = {"q": lambda bt: turn(bt, "q", 0, 0, TC), "qs": lambda bt: turn(bt, "qs", 1, 0, TS),
                      "k": lambda bt: turn(bt, "k", 2, 1, TC), "ks": lambda bt: turn(bt, "ks", 3, 1, TS),
                      "proj": add_attention, "logits": clip_logits}

            dve.wait_ge(x_first, 16)
            statistics([X[:, t, :] for t in range(TB)], ST[:, 0:TB], MV[:, 0:TB], ln_stats)
            dve.wait_ge(ln_rstd, 1)
            for t in range(TB):
                last = dve.tensor_scalar(XN[:, t, :], X[:, t, :], MV[:, t, 0:1], RSTD[:, t:t + 1], ALU.subtract, ALU.mult)
            last.then_inc(xn_ready, 1)
            for i in range(2):
                dve.memset(VP[i][:, :], 1.0).then_inc(built, 1)
            dve.wait_ge(ident_loaded, 16)
            dve.tensor_copy(IDB[:, :], IDF[:, :])
            dve.wait_ge(weights, 48)

            def first_turn(i):
                dve.wait_ge(first_full, i + 1)
                if i == 2:
                    dve.wait_ge(resid[0], 1)
                last = dve.tensor_tensor((TC, TS)[i % 2][:, :], FIRSTB[i], ROPE[:, i, :], ALU.mult)
                if i % 2 == 1:
                    last.then_inc(first_turned, 1)

            def first_sum(w):
                dve.wait_ge(first_turned, w + 1)
                dve.tensor_tensor(RES[w][:, :], TC[:, :], TS[:, :], ALU.add).then_inc(resid[w], 1)

            def first_cut(w, i):
                dve.wait_ge(resid[w], i + 1)
                dve.tensor_copy(PARTS[w][:, i, :], RES[w][:, :]).then_inc(part[w], 1)

            def first_subtract(w, i):
                dve.wait_ge(part[w], i + 1)
                dve.tensor_tensor(RES[w][:, :], RES[w][:, :], PARTS[w][:, i, :], ALU.subtract).then_inc(resid[w], 1)

            first_turn(0)
            first_turn(1)
            first_sum(0)
            first_cut(0, 0)
            first_subtract(0, 0)
            first_turn(2)
            first_cut(0, 1)
            first_subtract(0, 1)
            first_turn(3)
            first_cut(0, 2)
            first_sum(1)
            first_cut(1, 0)
            first_subtract(1, 0)
            first_cut(1, 1)
            first_subtract(1, 1)
            first_cut(1, 2)
            dve.wait_ge(tables, 32)
            dve.tensor_copy(RANKC[:, :], SMALL[:, T:T + 2 * B * E - 2])
            dve.tensor_copy(TOKEN[:, :], SMALL[:, 0:T])
            dve.wait_ge(x_rest, 16 * (B - 1))
            statistics([X[:, t, :] for t in range(TB, B * TB)], ST[:, TB:], MV[:, TB:], ln_stats)
            for u in range(NU):
                row_maxima(0, 0, u)

            def one(bt):
                b, par = bt.b, bt.par
                for s in range(4):
                    nb, npar, ns = (b, par, s + 1) if s < 3 else (b + 1, 1 - par, 0)
                    has_next, has_values = s < 3 or bt.nxt, s > 0 or bt.prev
                    for kind, i in STEP:
                        if kind == "u" and has_next:
                            row_maxima(nb, ns, i)
                        elif kind == "n":
                            minus_max(b, s, i)
                        elif kind == "ot" and has_values:
                            out_taken(bt, (s - 1) % 4)
                        elif kind == "x" and bt.extra(s, i) in extras:
                            extras[bt.extra(s, i)](bt)
                        if bt.nxt and (s, kind, i) in CUT_V:
                            cut(bt.b + 1, *CUT_V[s, kind, i])
                        if bt.prev and (s, kind, i) == STATISTICS2:
                            statistics2(bt)

            batches(dve, one)
            end = Batch(B, 0, order=MISC_END)
            out_taken(end, 3)
            add_attention(end)
            statistics2(end)
            clip_logits(end)
            dve.drain()

            def per_token(v):
                return v[:, :].rearrange("p (b t) -> p b t", b=B).unsqueeze(3).to_broadcast([P, B, TB, E])
            def halves(h):
                n = B // 2
                bs = slice(n * h, n * h + n)
                return (KT[:, bs, :, :], SCALED[:, bs, :, :],
                        PROD[:, h, :, :].rearrange("p t (b e) -> p b t e", b=n),
                        RINV[:, n * TB * h:n * TB * h + n * TB], RSC[:, n * TB * h:n * TB * h + n * TB], CSC[:, bs, :])

            def rows(v):
                return v.rearrange("p (b t) -> p b t", t=TB).unsqueeze(3).to_broadcast([P, B // 2, TB, E])
            lg4 = LG[:, :, :].rearrange("p (b t) e -> p b t e", b=B)
            dve.tensor_reduce(out=RSC[:, :], in_=LG[:, :, :], axis=AX.X, op=ALU.max)
            dve.drain()
            dve.reciprocal(RINV[:, :], RSC[:, :])
            dve.drain()
            dve.tensor_tensor(KT[:, :, :, :], lg4, per_token(RINV), ALU.mult)
            dve.drain()
            for h in range(2):
                kt, _, prod, _, rsc, _ = halves(h)
                dve.tensor_tensor(prod, kt, rows(rsc), ALU.mult).then_inc(sink_prod[h], 1)

            def rescale(i, h, steps, last=False):
                kt, scaled, prod, rinv, rsc, csc = halves(h)
                csum = CSUM[:, B // 2 * h:B // 2 * h + B // 2, :]
                gates = GATES[:, :, B // 2 * h:B // 2 * h + B // 2, :].rearrange("p t b e -> p b t e")
                for step in steps:
                    if step == 0:
                        dve.wait_ge(sink_sum[h], i + 1)
                        blocks = SUMS[h][:, 0:TB * B * E // 2].rearrange("p (t b e) -> p b e t", t=TB, e=E)
                        dve.tensor_reduce(out=csum, in_=blocks, axis=AX.X, op=ALU.add).then_inc(sink_step[h], 1)
                    elif step == 1:
                        dve.wait_ge(sink_step[h], 5 * i + 1)
                        dve.reciprocal(csc, csum).then_inc(sink_step[h], 1)
                    elif step == 2:
                        dve.wait_ge(sink_step[h], 5 * i + 2)
                        dve.tensor_tensor(scaled, kt, csc.unsqueeze(2).to_broadcast([P, B // 2, TB, E]),
                                          ALU.mult).then_inc(sink_step[h], 1)
                    elif step == 3:
                        dve.wait_ge(sink_step[h], 5 * i + 3)
                        dve.tensor_reduce(out=rinv, in_=scaled.rearrange("p b t e -> p (b t) e"),
                                          axis=AX.X, op=ALU.add).then_inc(sink_step[h], 1)
                    elif step == 4:
                        dve.wait_ge(sink_step[h], 5 * i + 4)
                        dve.reciprocal(rsc, rinv).then_inc(sink_step[h], 1)
                    else:
                        dve.wait_ge(sink_step[h], 5 * i + 5)
                        dve.tensor_tensor(gates if last else prod, scaled if last else kt, rows(rsc),
                                          ALU.mult).then_inc(sink_prod[h], 1)

            def half_steps(i, last=False):
                for step in range(3):
                    rescale(i, 0, [step])
                    rescale(i - 1, 1, [step + 3])
                rescale(i, 0, [3, 4, 5], last)
                rescale(i, 1, [0, 1, 2])

            rescale(0, 0, range(6))
            rescale(0, 1, range(3))
            with dve.Fori(1, SINKHORN_ITERS - 1) as i:
                half_steps(i)
            half_steps(SINKHORN_ITERS - 1, True)
            rescale(SINKHORN_ITERS - 1, 1, [3, 4, 5], True)

            dve.wait_ge(gt_ready, 1)
            dve.tensor_copy(GT[0][:, :], CH[2][0:B * E, :])
            dve.drain()
            ROUNDS = TOPK // 8
            for r in range(ROUNDS):
                if r > 0:
                    dve.wait_ge(top_removed, r)
                dve.max(out=TOPV[r % 2][:, :], in_=GT[r % 2][:, :]).then_inc(top_found, 1)
                dve.wait_ge(top_found, r + 1)
                if r < ROUNDS - 1:
                    if r > 0:
                        dve.wait_ge(top_placed, r)
                    dve.match_replace(out=GT[1 - r % 2][:, :], in_to_replace=TOPV[r % 2][:, :], in_values=GT[r % 2][:, :],
                                      imm_value=-1.0).then_inc(top_removed, 1)
                dve.max_index(out=TOPI[:, 8 * r:8 * r + 8], in_max=TOPV[r % 2][:, :], in_values=GT[r % 2][:, :]
                              ).then_inc(top_placed, 1)
            dve.wait_ge(top_placed, ROUNDS)
            dve.tensor_copy(TOPF[:, 0, :], TOPI[:, :])
            dve.tensor_copy(TOPF[:, 1, :], TOPI[:, :]).then_inc(topi_ready, 1)
            dve.wait_ge(it_ready, 1)
            for half in range(2):
                dve.tensor_copy(IT[64 * half:64 * half + 64, :],
                                MB[64 * half:64 * half + 64, 0:B * E].rearrange("p (c h) -> p c h", h=2)[:, :, half])
            dve.drain()
            with dve.Fori(0, B) as b:
                for e2 in range(E // 2):
                    dve.wait_ge(onehot_used, 4 * b + e2 + 1)
                    dve.tensor_scalar(OH[e2][:, :], TOKEN[:, :], IT[:, bass.ds(4 * b + e2, 1)], None,
                                      ALU.is_equal).then_inc(onehot, 1)

            dve.wait_ge(onehot_used, 4 + 4 * B)
            dve.tensor_copy(RT[:, :], ROWP[2][0:B * E, :]).then_inc(rt_ready, 1)
            dve.wait_ge(ranks_turned, 1)
            numbers = SMALL[:, T + 2 * B * E - 2:T + 2 * B * E - 2 + E].unsqueeze(1).to_broadcast([P, TB * B, E])
            dve.scalar_tensor_tensor(out=KEY[:, :, :], in0=MB[:, 0:TB * B * E].rearrange("p (t e) -> p t e", e=E),
                                     scalar=float(E), in1=numbers, op0=ALU.mult, op1=ALU.add)
            dve.tensor_scalar(OPEN[:, :, :], GATES[:, :, :, :].rearrange("p t b e -> p (t b) e"), 0.5, None, ALU.is_gt)
            dve.drain()
            dve.tensor_reduce(out=KMAX[:, :], in_=KEY[:, :, :], axis=AX.X, op=ALU.max)
            dve.scalar_tensor_tensor(out=OPEN[:, :, :], in0=KEY[:, :, :], scalar=float(E), in1=OPEN[:, :, :],
                                     op0=ALU.is_ge, op1=ALU.mult)
            dve.drain()
            dve.tensor_tensor(HARD[:, :, :], KEY[:, :, :], KMAX[:, :].unsqueeze(2).to_broadcast([P, TB * B, E]),
                              ALU.is_equal)
            dve.drain()
            dve.tensor_tensor(W[:, :], HARD[:, :, :].rearrange("p t e -> p (t e)"),
                              OPEN[:, :, :].rearrange("p t e -> p (t e)"), ALU.mult).then_inc(w_ready, 1)
            dve.drain()

            own = [(b, t) for b in range(DIRECT) for t in SHARE[b]]
            direct = [(b, t) for b in range(DIRECT, B) for t in range(TB)]
            tiles = direct + own
            done = 0
            for first in range(0, len(tiles), 2):
                pair = tiles[first:first + 2]
                for e in range(E):
                    for b, t in pair:
                        n, x = TB * b + t, X[:, TB * b + t, :]
                        if e > 0:
                            dve.wait_ge(chain, done - len(pair) + 1)
                        elif b >= DIRECT:
                            dve.wait_ge(y_full, n + 1)
                        else:
                            dve.wait_ge(y_copied, n + 1)
                        y = outputs(n, e) if b < DIRECT else DIRECTB[n % 4][e // 4][:, C * (e % 4):C * (e % 4) + C]
                        dve.scalar_tensor_tensor(out=x, in0=y, scalar=weight(b, t, e), in1=x,
                                                 op0=ALU.mult, op1=ALU.add).then_inc(chain, 1)
                        done += 1


_OUT = (B, T, C)


def _layout():
    half, d, pair = np.meshgrid(np.arange(2), np.arange(HD), np.arange(PAIRS), indexing="ij")
    cols = ((2 * pair + half) * HD + d).reshape(-1)
    swap = ((2 * pair + half) * HD + (d ^ 1)).reshape(-1)
    inv = (np.float32(1.0) / np.float32(10000.0) ** (np.arange(0, HD, 2, dtype=np.float32) / np.float32(HD)))
    freqs = np.arange(T, dtype=np.float32)[:, None] * inv.astype(np.float32)[None, :]
    cos, sin = np.cos(freqs).astype(np.float32), np.sin(freqs).astype(np.float32)
    dd = d.reshape(-1)
    c = cos[:, dd // 2].T
    s = sin[:, dd // 2].T * np.where(dd % 2 == 0, -1.0, 1.0)[:, None].astype(np.float32)
    scale = np.float32(1.0) / np.sqrt(np.float32(HD))
    rope = np.stack([c * scale, s * scale, c, s], axis=1).astype(np.float32)
    tri = np.zeros((P, T), np.float32)
    q, k = np.meshgrid(np.arange(P), np.arange(P), indexing="ij")
    tri[:, T - P:] = np.where(k > q, np.float32(-3e38), np.float32(0))
    small = np.zeros((P, T + 2 * B * E - 2 + E), np.float32)
    small[:, 0:T] = np.arange(T)
    place = np.arange(P) % TOPK + 1
    small[:, T + MID] = np.where(np.arange(P) < TOPK, place, 0)
    small[:, T + MID + 1] = np.where(np.arange(P) >= TOPK, place, 0)
    small[:, T + 2 * B * E - 2:] = np.arange(E)
    return cols, swap, rope, tri, small


def kernel(L0_attn_x, L0_attn_W_attn, L0_attn_W_proj, L0_ffn_gate_w, L0_ffn_experts):
    import concourse.bacc as _bacc
    from concourse.bass_utils import run_bass_kernel_spmd as _run

    cols, swap, rope, tri, small = _layout()
    w = np.asarray(L0_attn_W_attn)
    arrays = {
        "x": np.ascontiguousarray(L0_attn_x),
        "w_qkv": np.ascontiguousarray(np.concatenate([w[:, cols], w[:, C + cols], w[:, 2 * C:]], axis=1)),
        "w_swap": np.ascontiguousarray(np.concatenate([w[:, swap], w[:, C + swap]], axis=1)),
        "w_proj": np.ascontiguousarray(L0_attn_W_proj),
        "gate_w": np.ascontiguousarray(np.asarray(L0_ffn_gate_w)[0]),
        "experts": np.ascontiguousarray(L0_ffn_experts),
        "rope": rope, "tri": tri, "ident": np.eye(P, dtype=np.float32), "small": small,
    }
    nc = _bacc.Bacc("TRN2", target_bir_lowering=False, num_devices=1)
    args = [nc.dram_tensor(f"in_{name}", a.shape, mybir.dt.from_np(a.dtype), kind="ExternalInput").ap()
            for name, a in arrays.items()]
    out = nc.dram_tensor("out_0", _OUT, F32, kind="ExternalOutput").ap()
    build(nc, *args, out)
    r = _run(nc, [{f"in_{name}": a for name, a in arrays.items()}], core_ids=[0])
    return r.results[0]["out_0"]
```
